# Optimizing a Trainium2 kernel written in Bass

```python
import numpy as np
import jax
import jax.numpy as jnp

def _softmax(x, axis=-1):
    return jax.nn.softmax(x, axis=axis)

def _gelu(x):
    return jax.nn.gelu(x, approximate=True)

def _silu(x):
    return jax.nn.silu(x)

def _sigmoid(x):
    return jax.nn.sigmoid(x)

def _layernorm(x, axis=-1, eps=1e-05):
    m = jnp.mean(x, axis=axis, keepdims=True)
    v = jnp.var(x, axis=axis, keepdims=True)
    return (x - m) / jnp.sqrt(v + eps)

def _scatter_add(tgt, idx, src, axis=0):
    return tgt.at[idx].add(src)

def _segment_sum(src, seg, n):
    return jax.ops.segment_sum(src, seg, n)
kernel_name = 'mk_prb_d1_jaxref_r8_b9cc6a'

def setup_inputs(seed: int=0):
    np.random.seed(seed)
    _w = jnp.asarray

    def _L0_attn_setup():
        import jax, jax.numpy as jnp
        import numpy as np
        DIN = 128
        DOUT = 128
        key = jax.random.key(seed)
        kx, kq, kk, kv = jax.random.split(key, 4)
        B, T = (4, 256)
        x = jax.random.normal(kx, (B, T, DIN), dtype=jnp.float32)
        s = 1.0 / np.sqrt(DIN)
        Wq = jax.random.uniform(kq, (DOUT, DIN), minval=-s, maxval=s, dtype=jnp.float32)
        Wk = jax.random.uniform(kk, (DOUT, DIN), minval=-s, maxval=s, dtype=jnp.float32)
        Wv = jax.random.uniform(kv, (DOUT, DIN), minval=-s, maxval=s, dtype=jnp.float32)
        return {'x': x, 'Wq': Wq, 'Wk': Wk, 'Wv': Wv}
    _L0_attn_in = _L0_attn_setup()

    def _L0_ffn_setup():
        import jax, jax.numpy as jnp
        import numpy as np
        key = jax.random.key(seed)
        k1, k2, k3 = jax.random.split(key, 3)
        B, S, D, E, H = (4, 256, 128, 8, 128)
        x = jax.random.normal(k1, (B, S, D), dtype=jnp.float32)
        Wg = jax.random.normal(k2, (D, E), dtype=jnp.float32) / np.sqrt(D)
        We = jax.random.normal(k3, (E, D, H), dtype=jnp.float32) / np.sqrt(D)
        be = jnp.zeros((E, H), dtype=jnp.float32)
        return {'x': x, 'Wg': Wg, 'We': We, 'be': be}
    _L0_ffn_in = _L0_ffn_setup()
    _d = {'L0_attn_x': _L0_attn_in['x'], 'L0_attn_Wq': _L0_attn_in['Wq'], 'L0_attn_Wk': _L0_attn_in['Wk'], 'L0_attn_Wv': _L0_attn_in['Wv'], 'L0_ffn_Wg': _L0_ffn_in['Wg'], 'L0_ffn_We': _L0_ffn_in['We'], 'L0_ffn_be': _L0_ffn_in['be']}
    _x0 = _d['L0_attn_x']
    _d['L0_attn_x'] = jax.random.normal(jax.random.fold_in(jax.random.key(seed), 1), (8, 512, 128), dtype=_x0.dtype)
    del _x0
    return _d

def reference(L0_attn_x, L0_attn_Wq, L0_attn_Wk, L0_attn_Wv, L0_ffn_Wg, L0_ffn_We, L0_ffn_be):

    def _L0_attn_ref(x, Wq, Wk, Wv):
        import jax, jax.numpy as jnp
        import numpy as np
        DIN = 128
        DOUT = 128
        B, T, _ = x.shape
        q = jnp.einsum('btd,ed->bte', x, Wq)
        k = jnp.einsum('btd,ed->bte', x, Wk)
        v = jnp.einsum('btd,ed->bte', x, Wv)
        attn = jnp.einsum('bqe,bke->bqk', q, k)
        mask = jnp.tril(jnp.ones((T, T), dtype=attn.dtype))
        attn = attn * mask
        attn = jax.nn.softmax(attn / jnp.sqrt(jnp.asarray(T, attn.dtype)), axis=-1)
        return jnp.einsum('bqk,bke->bqe', attn, v)

    def _L0_ffn_ref(x, Wg, We, be):
        import jax, jax.numpy as jnp
        import numpy as np
        B, S, D = x.shape
        E = Wg.shape[1]
        T = B * S
        xf = x.reshape(T, D)
        gates = jax.nn.softmax(xf @ Wg, axis=-1)
        top_g, top_i = jax.lax.top_k(gates, 2)
        top_g = top_g / jnp.sum(top_g, axis=-1, keepdims=True)
        tok = jnp.arange(T)
        dispatch = jnp.zeros((E, T), dtype=gates.dtype)
        for i in range(2):
            dispatch = dispatch.at[top_i[:, i], tok].add(top_g[:, i])
        y = jnp.einsum('td,edh->eth', xf, We) + be[:, None, :]
        out = jnp.einsum('et,eth->th', dispatch, y)
        return out.reshape(B, S, -1)
    x = L0_attn_x
    xn = _layernorm(x, axis=-1)
    x = x + _L0_attn_ref(xn, L0_attn_Wq, L0_attn_Wk, L0_attn_Wv) + _L0_ffn_ref(xn, L0_ffn_Wg, L0_ffn_We, L0_ffn_be)
    return x

_drawn_inputs = setup_inputs


def setup_inputs(seed=0):
    import zlib

    import numpy as np

    out = dict(_drawn_inputs(seed))
    spreads = {'L0_ffn_be': (0.0, 0.1)}
    factors = {'L0_attn_Wq': 8.0, 'L0_attn_Wk': 8.0, 'L0_attn_Wv': 2.834}
    for name, (base, spread) in spreads.items():
        noise = np.random.default_rng([zlib.crc32(name.encode()), seed]).standard_normal(out[name].shape)
        drawn = base * np.exp(spread * noise) if base else spread * noise
        out[name] = jnp.asarray(drawn.astype(out[name].dtype))
    for name, factor in factors.items():
        out[name] = (out[name] * factor).astype(out[name].dtype)
    return out
```

```python
from contextlib import ExitStack

import concourse.bass as bass
from concourse import mybir

F32 = mybir.dt.float32
F32R = mybir.dt.float32r
U32 = mybir.dt.uint32
ALU = mybir.AluOpType
ACT = mybir.ActivationFunctionType
AX_X = mybir.AxisListType.X

P = 128
EPS = 1e-5
GROUPS = "C0 A0 B0 C1 A1 B1 V0 C2 A2 B2 V1 C3 A3 B3 X SV V2 U V3 BI".split()
RING = 5
C_COLS, AB_COLS = 2 * P + P + 8, 3 * P
OFF = {"C": 0, "A": C_COLS, "B": C_COLS + AB_COLS}
V_AT, G_AT = 2 * P, 3 * P
ROWS = 32
E_ROW = 24


class Chain:

    def __init__(self, engine, sem):
        self.engine, self.sem, self.n, self.base = engine, sem, 0, 0

    def step(self, instruction):
        self.n += 1
        instruction.then_inc(self.sem, 1)
        self.engine.wait_ge(self.sem, self.base + self.n)


def build(nc, x, Wq, Wk, Wv, Wg, We, be, rows, pick, out, looped=True):
    B, T, D = x.shape
    E = Wg.shape[1]
    NT = T // P
    assert D == P and NT == 4 and E == 8
    SCALE = float(T) ** -0.5
    NW = E * P + P + E

    x_v = x.rearrange("b (t p) d -> b p t d", p=P)
    out_v = out.rearrange("b (t p) d -> b p t d", p=P)

    with ExitStack() as ctx:
        def sb(name, shape, dt=F32):
            return ctx.enter_context(nc.sbuf_tensor(name, shape, dt))

        def ps(name):
            return ctx.enter_context(nc.psum_tensor(name, [P, 512], F32))

        def sem(name):
            return ctx.enter_context(nc.semaphore(name))

        wq_s, wk_s, wv_s = (sb(n, [P, P]) for n in ("wq_s", "wk_s", "wv_s"))
        w_f = sb("w_f", [P, NW])
        w_hi, w_lo = (sb(n, [P, NW], F32R) for n in ("w_hi", "w_lo"))
        a_hi, a_lo = (sb(n, [P, P], F32R) for n in ("a_hi", "a_lo"))
        be_s = sb("be_s", [E, P])
        rows_s = sb("rows_s", [P, 1])
        pick_s = sb("pick_s", [E, P])
        be_rows = sb("be_rows", [P, P], F32R)
        ident = sb("ident", [P, P])
        causal = sb("causal", [P, P])
        suffix = sb("suffix", [P, NT, P])
        iota8 = sb("iota8", [P, E])
        half = sb("half", [P, NT])
        ones = sb("ones", [P, NT, 2, E])
        x_all = sb("x_all", [P, B * NT * P])
        stats = sb("stats", [P, NT, 6])
        mv = sb("mv", [P, NT, 2])
        veps, rstd, nmean, nmr = (sb(n, [P, NT]) for n in ("veps", "rstd", "nmean", "nmr"))
        xn = sb("xn", [P, NT, P])
        xT_hi, xT_lo, uT_hi, uT_lo = (sb(n, [P, NT * P], F32R) for n in ("xT_hi", "xT_lo", "uT_hi", "uT_lo"))
        v_s = sb("v_s", [P, NT, P + E])
        prob = sb("prob", [P, 2, NT * P])
        probT = sb("probT", [P, 2, NT * P])
        mx, nmx, em, rs, tot, rinv, en = (sb(n, [P, NT]) for n in ("mx", "nmx", "em", "rs", "tot", "rinv", "en"))
        top8 = sb("top8", [P, E])
        idx8 = sb("idx8", [P, E], U32)
        nm1, gsum, grec = (sb(n, [P, 1]) for n in ("nm1", "gsum", "grec"))
        gexp, first, picked, gnum = (sb(n, [P, E]) for n in ("gexp", "first", "picked", "gnum"))
        gate = sb("gate", [P, NT, E])
        ysc = sb("ysc", [P, 2, E, P])
        ffn = sb("ffn", [P, NT, P])
        lhs_rows = sb("lhs_rows", [P, NT * ROWS], F32R)
        lhsT_rows = sb("lhsT_rows", [P, P], F32R)
        sv_hi = sb("sv_hi", [P, P], F32R)
        rhs_rows = sb("rhs_rows", [P, NT, P], F32R)
        sv_rows = sb("sv_rows", [P, P], F32R)
        o_s = sb("o_s", [P, NT, P])

        ring = [ps(f"ring{i}") for i in range(RING)]
        score = [ps("score0"), ps("score1")]
        ptb = ps("ptb")

        names = """w_att w_moe w_const x0 x1 x_rest a_done wvt_done a_ready w_ready be_done be_ready
            wide_done scores_done pt_done pv_done xt_done sv_done dt_done u_done bias_done
            v_ready gexp_ready c_used a_used b_used exp_done em_done pt_ready xn_ready xh_ready xl_ready uh_ready
            ul_ready svh_ready rhs_ready dt_ready veps_ready nmean_ready rstd_ready stats_ready nm1_ready gate_ready nmx_ready
            rinv_ready fin_done out_ready rows_ready ffn_ready sv_rows_ready stored dve_chain act_chain pool_chain
            dummy setup_hi half_ready ident_ready consts_ready"""
        S = {n: sem(n) for n in names.split()}

        block = ctx.enter_context(nc.Block())

        def tile_ap(b, t):
            return x_all[:, bass.ds(b * (NT * P) + t * P, P)]

        def bank(g):
            return ring[GROUPS.index(g) % RING]

        def steady(eng, body, last=B - 1):
            body(0)
            if looped:
                with eng.Fori(1, last) as b:
                    body(b)
            else:
                for b in range(1, last):
                    body(b)
            body(last)

        def steady_chain(eng, body, chain):
            start = chain.n
            chain.base, chain.n = start, 0
            body(0)
            per = chain.n
            if looped:
                with eng.Fori(1, B - 1) as b:
                    chain.base, chain.n = b * per + start, 0
                    body(b)
            else:
                for b in range(1, B - 1):
                    chain.base, chain.n = b * per + start, 0
                    body(b)
            chain.base, chain.n = (B - 1) * per + start, 0
            body(B - 1)

        def is_first(b):
            return isinstance(b, int) and b == 0

        def is_last(b):
            return isinstance(b, int) and b == B - 1

        @block.sync
        def _(sp):
            sp.dma_start(x_all[:, 0:NT * P].rearrange("p (t d) -> p t d", d=P), x_v[0]).then_inc(S["x0"], 16)
            sp.dma_start(wq_s[:], Wq).then_inc(S["w_att"], 16)
            sp.dma_start(wk_s[:], Wk).then_inc(S["w_att"], 16)
            sp.dma_start(w_f[:, OFF["A"]:OFF["A"] + 6 * P].rearrange("p (e h) -> p e h", h=P),
                         We[0:6].rearrange("e d h -> d e h")).then_inc(S["w_moe"], 16)
            sp.dma_start(x_all[:, NT * P:2 * NT * P].rearrange("p (t d) -> p t d", d=P), x_v[1]).then_inc(S["x1"], 16)
            for b in range(2, B):
                sp.dma_start(x_all[:, b * NT * P:(b + 1) * NT * P].rearrange("p (t d) -> p t d", d=P),
                             x_v[b]).then_inc(S["x_rest"], 16)

            def store(b):
                sp.wait_ge(S["out_ready"], b + 1)
                sp.dma_start(out_v[b].rearrange("p t d -> p t d"), o_s[:, :, :]).then_inc(S["stored"], 16)

            for b in range(B):
                store(b)
            sp.wait_ge(S["stored"], 16 * B)

        @block.tensor
        def _(pe):
            def ring_free(g, b):
                n = GROUPS.index(g) - RING
                if n < 0 and is_first(b):
                    if GROUPS[n] == "U":
                        pe.wait_ge(S["uh_ready"], 1)
                        pe.wait_ge(S["ul_ready"], 1)
                    return
                if n < 0:
                    b = b - 1
                prev = GROUPS[n % len(GROUPS)]
                if prev in "XU" and is_last(b):
                    return
                k, t = prev[0], prev[1:]
                if prev == "X":
                    pe.wait_ge(S["xh_ready"], b + 2)
                    pe.wait_ge(S["xl_ready"], b + 2)
                elif prev == "U":
                    pe.wait_ge(S["uh_ready"], b + 2)
                    pe.wait_ge(S["ul_ready"], b + 2)
                elif prev == "SV":
                    pe.wait_ge(S["sv_rows_ready"], b + 1)
                elif prev == "BI":
                    pe.wait_ge(S["out_ready"], b + 1)
                else:
                    pe.wait_ge(S[{"C": "c_used", "A": "a_used", "B": "b_used", "V": "fin_done"}[k]], NT * b + int(t) + 1)

            def three(dst, hi, lo, w_h, w_l):
                nc.tensor.matmul(dst, hi, w_h, start=True, stop=False)
                nc.tensor.matmul(dst, hi, w_l, start=False, stop=False)
                return nc.tensor.matmul(dst, lo, w_h, start=False, stop=True)

            def wide(k, b, t):
                ring_free(f"{k}{t}", b)
                n = C_COLS if k == "C" else AB_COLS
                c = slice(OFF[k], OFF[k] + n)
                r = slice(t * P, (t + 1) * P)
                three(bank(f"{k}{t}")[:, 0:n], xT_hi[:, r], xT_lo[:, r], w_hi[:, c], w_lo[:, c]
                      ).then_inc(S["wide_done"], 1)

            def scores(b, t):
                if t == 0:
                    pe.wait_ge(S["uh_ready"], b + 1)
                    pe.wait_ge(S["ul_ready"], b + 1)
                if not (is_first(b) and t < 2):
                    pe.wait_ge(S["exp_done"], b * NT + t - 1)
                r, n = slice(t * P, (t + 1) * P), (t + 1) * P
                three(score[t % 2][:, 0:n], uT_hi[:, r], uT_lo[:, r], xT_hi[:, 0:n], xT_lo[:, 0:n]
                      ).then_inc(S["scores_done"], 1)

            def transpose_probs(b, t):
                pe.wait_ge(S["exp_done"], b * NT + t + 1)
                if not (is_first(b) and t == 0):
                    pe.wait_ge(S["pt_ready"], b * NT + t)
                if t == NT - 1:
                    pe.wait_ge(S["dt_ready"], b + 1)
                for j in range(t + 1):
                    last = nc.tensor.transpose(ptb[:, j * P:(j + 1) * P], prob[:, t % 2, j * P:(j + 1) * P], ident[:])
                last.then_inc(S["pt_done"], 1)

            def attend(b, t):
                pe.wait_ge(S["pt_ready"], b * NT + t + 1)
                pe.wait_ge(S["v_ready"], b * NT + t + 1)
                ring_free(f"V{t}", b)
                for j in range(t + 1):
                    last = nc.tensor.matmul(bank(f"V{t}")[:, 0:P], probT[:, t % 2, j * P:(j + 1) * P],
                                            v_s[:, j, 0:P], start=(j == 0), stop=(j == t))
                last.then_inc(S["pv_done"], 1)

            def transpose_x(b, ready):
                pe.wait_ge(S["xn_ready"], ready)
                for t in range(NT):
                    last = nc.tensor.transpose(bank("X")[:, t * P:(t + 1) * P], xn[:, t, :], ident[:])
                last.then_inc(S["xt_done"], 1)

            def project_u(ready):
                pe.wait_ge(S["xh_ready"], ready)
                pe.wait_ge(S["xl_ready"], ready)
                dst = bank("U")[:, :]
                nc.tensor.matmul(dst, a_hi[:], xT_hi[:], start=True, stop=False)
                nc.tensor.matmul(dst, a_lo[:], xT_hi[:], start=False, stop=False)
                nc.tensor.matmul(dst, a_hi[:], xT_lo[:], start=False, stop=True).then_inc(S["u_done"], 1)

            def value_sums(b):
                ring_free("SV", b)
                pe.wait_ge(S["v_ready"], b * NT + NT)
                for m in range(1, NT):
                    last = nc.tensor.matmul(bank("SV")[:, 0:P], suffix[:, m, :], v_s[:, m, 0:P],
                                            start=(m == 1), stop=(m == NT - 1))
                last.then_inc(S["sv_done"], 1)

            def transpose_rows(b):
                pe.wait_ge(S["rows_ready"], b + 1)
                pe.wait_ge(S["pt_ready"], b * NT + 3)
                nc.tensor.transpose(ptb[:, 0:P], lhs_rows[:].bitcast(F32), ident[:]).then_inc(S["dt_done"], 1)

            def bias(b):
                ring_free("BI", b)
                pe.wait_ge(S["rhs_ready"], b + 1)
                pe.wait_ge(S["dt_ready"], b + 1)
                nc.tensor.matmul(bank("BI")[:, :], lhsT_rows[:], rhs_rows[:].rearrange("p t h -> p (t h)"),
                                 start=True, stop=True).then_inc(S["bias_done"], 1)

            pe.wait_ge(S["w_att"], 32)
            nc.tensor.matmul(score[0][:, 0:P], wq_s[:], wk_s[:], start=True, stop=True).then_inc(S["a_done"], 1)
            pe.wait_ge(S["ident_ready"], 1)
            transpose_x(0, NT)
            pe.wait_ge(S["w_const"], 80)
            nc.tensor.transpose(ring[0][:, 0:P], wv_s[:], ident[:]).then_inc(S["wvt_done"], 1)
            nc.tensor.matmul(ptb[:, 0:P], pick_s[:], be_s[:], start=True, stop=True).then_inc(S["be_done"], 1)
            pe.wait_ge(S["a_ready"], 1)
            project_u(1)
            pe.wait_ge(S["w_ready"], 2)
            pe.wait_ge(S["be_ready"], 1)
            pe.wait_ge(S["consts_ready"], 1)

            def body(b):
                wide("C", b, 0)
                wide("A", b, 0)
                scores(b, 0)
                wide("B", b, 0)
                scores(b, 1)
                wide("C", b, 1)
                wide("A", b, 1)
                transpose_probs(b, 0)
                wide("B", b, 1)
                attend(b, 0)
                scores(b, 2)
                wide("C", b, 2)
                wide("A", b, 2)
                transpose_probs(b, 1)
                wide("B", b, 2)
                attend(b, 1)
                scores(b, 3)
                wide("C", b, 3)
                wide("A", b, 3)
                transpose_probs(b, 2)
                wide("B", b, 3)
                ring_free("X", b)
                if not is_last(b):
                    transpose_x(b, b * NT + 2 * NT)
                value_sums(b)
                attend(b, 2)
                transpose_rows(b)
                transpose_probs(b, 3)
                ring_free("U", b)
                if not is_last(b):
                    project_u(b + 2)
                attend(b, 3)
                bias(b)

            steady(pe, body)

        @block.vector
        def _(dve):
            chain = Chain(dve, S["dve_chain"])

            def normal_stats(b, tiles):
                for t in tiles:
                    nc.vector.bn_stats(stats[:, t, :], tile_ap(b, t)).then_inc(S["stats_ready"], 1)

            def normal_finish(b):
                dve.wait_ge(S["stats_ready"], b * NT + NT)
                dve.sem_inc(S["dummy"], 1)
                for t in range(NT):
                    last = nc.vector.bn_aggr(mv[:, t, :], stats[:, t, :])
                chain.step(last)
                if not is_first(b):
                    dve.wait_ge(S["rstd_ready"], b)
                nc.vector.tensor_scalar(nmean[:], mv[:, :, 0], -1.0, None, ALU.mult).then_inc(S["nmean_ready"], 1)
                nc.vector.tensor_scalar_add(veps[:], mv[:, :, 1], EPS).then_inc(S["veps_ready"], 1)

            def split_lo(dst, src, hi, done):
                nc.vector.tensor_tensor(dst, src, hi.bitcast(F32), ALU.subtract).then_inc(done, 1)

            def gates(b, t):
                lg = v_s[:, t, P:P + E]
                dve.wait_ge(S["v_ready"], b * NT + t + 1)
                dve.sem_inc(S["dummy"], 1)
                chain.step(nc.vector.max(top8[:], lg))
                nc.vector.tensor_scalar(nm1[:], top8[:, 0:1], -1.0, None, ALU.mult).then_inc(S["nm1_ready"], 1)
                chain.step(nc.vector.max_index(idx8[:], top8[:], lg))
                chain.step(nc.vector.tensor_scalar(first[:], iota8[:], idx8[:, 0:1], None, ALU.is_equal))
                chain.step(nc.vector.scalar_tensor_tensor(picked[:], iota8[:], idx8[:, 1:2], first[:],
                                                          ALU.is_equal, ALU.add))
                dve.wait_ge(S["gexp_ready"], b * NT + t + 1)
                chain.step(nc.vector.scalar_tensor_tensor(gnum[:], picked[:], 1.0, gexp[:], ALU.mult, ALU.mult,
                                                          accum_out=gsum[:]))
                chain.step(nc.vector.reciprocal(grec[:], gsum[:]))
                if t == 0 and not is_first(b):
                    dve.wait_ge(S["rows_ready"], b)
                nc.vector.tensor_scalar(gate[:, t, :], gnum[:], grec[:], None, ALU.mult).then_inc(S["gate_ready"], 1)

            def scale_b(b, t):
                dve.wait_ge(S["wide_done"], b * (3 * NT) + 3 * t + 3)
                dve.wait_ge(S["gate_ready"], b * NT + t + 1)
                if not (is_first(b) and t < 2):
                    dve.wait_ge(S["ffn_ready"], b * NT + t - 1)
                nc.vector.tensor_tensor(
                    ysc[:, t % 2, 3:6, :], bank(f"B{t}")[:, 0:AB_COLS].rearrange("p (e h) -> p e h", h=P),
                    gate[:, t, 3:6].unsqueeze(2).to_broadcast([P, 3, P]), ALU.mult).then_inc(S["b_used"], 1)

            def softmax_max(b, t):
                s = score[t % 2]
                dve.wait_ge(S["scores_done"], b * NT + t + 1)
                diag = s[:, t * P:(t + 1) * P]
                chain.step(nc.vector.tensor_tensor(diag, diag, causal[:], ALU.mult))
                chain.step(nc.vector.reduce_max(mx[:, t:t + 1], s[:, 0:(t + 1) * P], AX_X))
                if t == 0 and not is_first(b):
                    dve.wait_ge(S["exp_done"], b * NT)
                if t < NT - 1:
                    ins = nc.vector.tensor_scalar(nmx[:, t:t + 1], mx[:, t:t + 1], -SCALE, 0.0, ALU.mult, ALU.min)
                else:
                    ins = nc.vector.tensor_scalar(nmx[:, t:t + 1], mx[:, t:t + 1], -SCALE, None, ALU.mult)
                ins.then_inc(S["nmx_ready"], 1)

            def softmax_sum(b, t):
                dve.wait_ge(S["exp_done"], b * NT + t + 1)
                total = rs
                if t < NT - 1:
                    dve.wait_ge(S["em_done"], b * (NT - 1) + t + 1)
                    chain.step(nc.vector.scalar_tensor_tensor(tot[:, t:t + 1], em[:, t:t + 1], float(T - (t + 1) * P),
                                                              rs[:, t:t + 1], ALU.mult, ALU.add))
                    total = tot
                if t == 0 and not is_first(b):
                    dve.wait_ge(S["rows_ready"], b)
                nc.vector.reciprocal(rinv[:, t:t + 1], total[:, t:t + 1]).then_inc(S["rinv_ready"], 1)

            def finish_tile(b, t):
                dve.wait_ge(S["pv_done"], b * NT + t + 1)
                dve.wait_ge(S["rinv_ready"], b * NT + t + 1)
                dve.wait_ge(S["ffn_ready"], b * NT + t + 1)
                if t == 0 and not is_first(b):
                    dve.wait_ge(S["stored"], b * 16)
                nc.vector.scalar_tensor_tensor(o_s[:, t, :], bank(f"V{t}")[:, 0:P], rinv[:, t:t + 1], ffn[:, t, :],
                                               ALU.mult, ALU.add).then_inc(S["fin_done"], 1)

            dve.wait_ge(S["x0"], 16)
            normal_stats(0, range(NT))
            normal_finish(0)
            nc.vector.memset(half[:], -0.5).then_inc(S["half_ready"], 1)
            dve.wait_ge(S["xt_done"], 1)
            dve.wait_ge(S["xh_ready"], 1)
            split_lo(xT_lo[:], bank("X")[:], xT_hi[:], S["xl_ready"])
            dve.wait_ge(S["setup_hi"], 1)
            split_lo(a_lo[:], score[0][:, 0:P], a_hi[:], S["a_ready"])
            dve.wait_ge(S["setup_hi"], 2)
            nc.vector.scalar_tensor_tensor(be_rows[:], sv_hi[:].bitcast(F32), rows_s[:], ptb[:, 0:P],
                                           ALU.mult, ALU.add).then_inc(S["be_ready"], 1)
            dve.wait_ge(S["w_ready"], 1)
            split_lo(w_lo[:], w_f[:], w_hi[:], S["w_ready"])
            dve.wait_ge(S["u_done"], 1)
            dve.wait_ge(S["uh_ready"], 1)
            split_lo(uT_lo[:], bank("U")[:], uT_hi[:], S["ul_ready"])
            dve.wait_ge(S["consts_ready"], 1)

            def body(b):
                gates(b, 0)
                softmax_max(b, 0)
                scale_b(b, 0)
                softmax_max(b, 1)
                softmax_sum(b, 0)
                gates(b, 1)
                if not is_last(b):
                    dve.wait_ge(S["x1" if is_first(b) else "x_rest"], 16 if is_first(b) else 16 * (B - 2))
                    normal_stats(b + 1, (0, 1))
                scale_b(b, 1)
                finish_tile(b, 0)
                softmax_max(b, 2)
                softmax_sum(b, 1)
                gates(b, 2)
                if not is_last(b):
                    normal_stats(b + 1, (2, 3))
                    normal_finish(b + 1)
                scale_b(b, 2)
                finish_tile(b, 1)
                softmax_max(b, 3)
                softmax_sum(b, 2)
                gates(b, 3)
                softmax_sum(b, 3)
                scale_b(b, 3)
                if not is_last(b):
                    dve.wait_ge(S["xt_done"], b + 2)
                    dve.wait_ge(S["xh_ready"], b + 2)
                    split_lo(xT_lo[:], bank("X")[:], xT_hi[:], S["xl_ready"])
                dve.wait_ge(S["svh_ready"], b + 1)
                nc.vector.scalar_tensor_tensor(sv_rows[:], sv_hi[:].bitcast(F32), rows_s[:], bank("SV")[:, 0:P],
                                               ALU.mult, ALU.add).then_inc(S["sv_rows_ready"], 1)
                finish_tile(b, 2)
                if not is_last(b):
                    dve.wait_ge(S["u_done"], b + 2)
                    dve.wait_ge(S["uh_ready"], b + 2)
                    split_lo(uT_lo[:], bank("U")[:], uT_hi[:], S["ul_ready"])
                finish_tile(b, 3)
                dve.wait_ge(S["fin_done"], b * NT + NT)
                dve.wait_ge(S["bias_done"], b + 1)
                nc.vector.tensor_tensor(o_s[:].rearrange("p t d -> p (t d)"), o_s[:].rearrange("p t d -> p (t d)"),
                                        bank("BI")[:], ALU.add).then_inc(S["out_ready"], 1)

            steady_chain(dve, body, chain)

        @block.scalar
        def _(act):
            act.dma_start(wv_s[:], Wv).then_inc(S["w_const"], 16)
            act.dma_start(w_f[:, G_AT:G_AT + E], Wg).then_inc(S["w_const"], 16)
            act.dma_start(w_f[:, 0:2 * P].rearrange("p (e h) -> p e h", h=P),
                          We[6:8].rearrange("e d h -> d e h")).then_inc(S["w_moe"], 16)
            act.dma_start(be_s[:], be).then_inc(S["w_const"], 16)
            act.dma_start(rows_s[:], rows).then_inc(S["w_const"], 16)
            act.dma_start(pick_s[:], pick).then_inc(S["w_const"], 16)

            def normalize(b):
                act.wait_ge(S["rstd_ready"], b + 1)
                if not is_first(b):
                    act.wait_ge(S["xt_done"], b)
                for t in range(NT):
                    nc.scalar.activation(xn[:, t, :], tile_ap(b, t), ACT.Identity, bias=nmr[:, t:t + 1],
                                         scale=rstd[:, t:t + 1]).then_inc(S["xn_ready"], 1)

            def value_copy(b, t):
                act.wait_ge(S["wide_done"], b * (3 * NT) + 3 * t + 1)
                if t == 0 and not is_first(b):
                    act.wait_ge(S["pv_done"], b * NT)
                nc.scalar.copy(v_s[:, t, :], bank(f"C{t}")[:, V_AT:V_AT + P + E]).then_inc(S["v_ready"], 1)

            def gate_exp(b, t):
                act.wait_ge(S["v_ready"], b * NT + t + 1)
                act.wait_ge(S["nm1_ready"], b * NT + t + 1)
                if not (is_first(b) and t == 0):
                    act.wait_ge(S["gate_ready"], b * NT + t)
                nc.scalar.activation(gexp[:], v_s[:, t, P:P + E], ACT.Exp,
                                     bias=nm1[:]).then_inc(S["gexp_ready"], 1)

            def scale_experts(b, t):
                act.wait_ge(S["gate_ready"], b * NT + t + 1)
                if not (is_first(b) and t < 2):
                    act.wait_ge(S["ffn_ready"], b * NT + t - 1)
                for i, e in enumerate((6, 7)):
                    last = nc.scalar.mul(ysc[:, t % 2, e, :], bank(f"C{t}")[:, i * P:(i + 1) * P], gate[:, t, e:e + 1])
                last.then_inc(S["c_used"], 1)
                act.wait_ge(S["wide_done"], b * (3 * NT) + 3 * t + 2)
                for e in range(3):
                    last = nc.scalar.mul(ysc[:, t % 2, e, :], bank(f"A{t}")[:, e * P:(e + 1) * P], gate[:, t, e:e + 1])
                last.then_inc(S["a_used"], 1)

            def softmax_exp(b, t):
                act.wait_ge(S["nmx_ready"], b * NT + t + 1)
                if not (is_first(b) and t < 2):
                    act.wait_ge(S["pt_done"], b * NT + t - 1)
                if t == 0 and not is_first(b):
                    act.wait_ge(S["rows_ready"], b)
                n = (t + 1) * P
                nc.scalar.activation(prob[:, t % 2, 0:n], score[t % 2][:, 0:n], ACT.Exp, bias=nmx[:, t:t + 1],
                                     scale=SCALE, accum_out=rs[:, t:t + 1]).then_inc(S["exp_done"], 1)
                if t < NT - 1:
                    nc.scalar.activation(em[:, t:t + 1], nmx[:, t:t + 1], ACT.Exp).then_inc(S["em_done"], 1)

            def probs_copy(b, t):
                act.wait_ge(S["pt_done"], b * NT + t + 1)
                if not (is_first(b) and t < 2):
                    act.wait_ge(S["pv_done"], b * NT + t - 1)
                n = (t + 1) * P
                nc.scalar.copy(probT[:, t % 2, 0:n], ptb[:, 0:n]).then_inc(S["pt_ready"], 1)

            normalize(0)
            act.wait_ge(S["a_done"], 1)
            nc.scalar.copy(a_hi[:], score[0][:, 0:P]).then_inc(S["setup_hi"], 1)
            act.wait_ge(S["xt_done"], 1)
            nc.scalar.copy(xT_hi[:], bank("X")[:]).then_inc(S["xh_ready"], 1)
            act.wait_ge(S["be_done"], 1)
            nc.scalar.copy(sv_hi[:], ptb[:, 0:P]).then_inc(S["setup_hi"], 1)
            act.wait_ge(S["wvt_done"], 1)
            nc.scalar.copy(w_f[:, V_AT:V_AT + P], ring[0][:, 0:P]).then_inc(S["act_chain"], 1)
            act.wait_ge(S["act_chain"], 1)
            act.wait_ge(S["w_moe"], 32)
            act.wait_ge(S["w_const"], 80)
            nc.scalar.copy(w_hi[:], w_f[:]).then_inc(S["w_ready"], 1)
            act.wait_ge(S["u_done"], 1)
            nc.scalar.copy(uT_hi[:], bank("U")[:]).then_inc(S["uh_ready"], 1)

            def body(b):
                value_copy(b, 0)
                gate_exp(b, 0)
                scale_experts(b, 0)
                softmax_exp(b, 0)
                softmax_exp(b, 1)
                value_copy(b, 1)
                gate_exp(b, 1)
                probs_copy(b, 0)
                scale_experts(b, 1)
                softmax_exp(b, 2)
                value_copy(b, 2)
                gate_exp(b, 2)
                probs_copy(b, 1)
                scale_experts(b, 2)
                softmax_exp(b, 3)
                if not is_last(b):
                    normalize(b + 1)
                value_copy(b, 3)
                gate_exp(b, 3)
                probs_copy(b, 2)
                scale_experts(b, 3)
                if not is_last(b):
                    act.wait_ge(S["xt_done"], b + 2)
                    nc.scalar.copy(xT_hi[:], bank("X")[:]).then_inc(S["xh_ready"], 1)
                act.wait_ge(S["sv_done"], b + 1)
                if not is_first(b):
                    act.wait_ge(S["sv_rows_ready"], b)
                nc.scalar.copy(sv_hi[:], bank("SV")[:, 0:P]).then_inc(S["svh_ready"], 1)
                act.wait_ge(S["dt_done"], b + 1)
                if not is_first(b):
                    act.wait_ge(S["bias_done"], b)
                nc.scalar.copy(lhsT_rows[:], ptb[:, 0:P]).then_inc(S["dt_ready"], 1)
                probs_copy(b, 3)
                if not is_last(b):
                    act.wait_ge(S["u_done"], b + 2)
                    nc.scalar.copy(uT_hi[:], bank("U")[:]).then_inc(S["uh_ready"], 1)

            steady(act, body)

        @block.gpsimd
        def _(pool):
            chain = Chain(pool, S["pool_chain"])

            def normal_rstd(b):
                pool.wait_ge(S["veps_ready"], b + 1)
                if not is_first(b):
                    pool.wait_ge(S["xn_ready"], b * NT)
                pool.wait_ge(S["nmean_ready"], b + 1)
                chain.step(nc.gpsimd.tensor_tensor(rstd[:], veps[:], half[:], ALU.pow))
                nc.gpsimd.tensor_tensor(nmr[:], nmean[:], rstd[:], ALU.mult).then_inc(S["rstd_ready"], 1)

            def sum_experts(b, t):
                y = ysc[:, t % 2, :, :]
                pool.wait_ge(S["a_used"], b * NT + t + 1)
                pool.wait_ge(S["b_used"], b * NT + t + 1)
                chain.step(nc.gpsimd.tensor_tensor(y[:, 0:4, :], y[:, 0:4, :], y[:, 4:8, :], ALU.add))
                chain.step(nc.gpsimd.tensor_tensor(y[:, 0:2, :], y[:, 0:2, :], y[:, 2:4, :], ALU.add))
                chain.step(nc.gpsimd.tensor_tensor(y[:, 0, :], y[:, 0, :], y[:, 1, :], ALU.add))
                if not is_first(b):
                    pool.wait_ge(S["fin_done"], b * NT + t + 1 - NT)
                nc.gpsimd.tensor_tensor(ffn[:, t, :], y[:, 0, :], tile_ap(b, t), ALU.add).then_inc(S["ffn_ready"], 1)

            def bias_rows(b):
                rows3 = lhs_rows[:].rearrange("p (t r) -> p t r", r=ROWS)
                pool.wait_ge(S["gate_ready"], b * NT + NT)
                pool.wait_ge(S["rinv_ready"], b * NT + NT)
                if not is_first(b):
                    pool.wait_ge(S["dt_done"], b)
                g_in = gate[:].unsqueeze(2).to_broadcast([P, NT, 2, E])
                g_hi = rows3[:, :, 0:2 * E].rearrange("p t (c e) -> p t c e", e=E)
                chain.step(nc.gpsimd.tensor_tensor(g_hi, g_in, ones[:], ALU.mult))
                chain.step(nc.gpsimd.tensor_tensor(rows3[:, :, 2 * E:3 * E], gate[:],
                                                   rows3[:, :, 0:E].bitcast(F32), ALU.subtract))
                n = NT - 1
                m_in, r_in = (v[:, 0:n].unsqueeze(2).to_broadcast([P, n, 2]) for v in (em, rinv))
                chain.step(nc.gpsimd.tensor_tensor(en[:, 0:n], em[:, 0:n], rinv[:, 0:n], ALU.mult))
                chain.step(nc.gpsimd.tensor_tensor(rows3[:, 0:n, E_ROW:E_ROW + 2], m_in, r_in, ALU.mult))
                nc.gpsimd.tensor_tensor(rows3[:, 0:n, E_ROW + 2], en[:, 0:n], rows3[:, 0:n, E_ROW].bitcast(F32),
                                        ALU.subtract).then_inc(S["rows_ready"], 1)

            def bias_rhs(b):
                pool.wait_ge(S["sv_rows_ready"], b + 1)
                if not is_first(b):
                    pool.wait_ge(S["bias_done"], b)
                pool.wait_ge(S["ffn_ready"], b * NT + NT)
                for t in range(NT):
                    r = slice(t * ROWS, (t + 1) * ROWS)
                    ins = nc.gpsimd.tensor_tensor(rhs_rows[r, t, :], sv_rows[r, :].bitcast(F32),
                                                  be_rows[r, :].bitcast(F32), ALU.add)
                    if t < NT - 1:
                        chain.step(ins)
                ins.then_inc(S["rhs_ready"], 1)
                pool.wait_ge(S["rhs_ready"], b + 1)

            chain.step(nc.gpsimd.memset(ones[:], 1.0))
            chain.step(nc.gpsimd.memset(ident[:], 0.0))
            nc.gpsimd.affine_select(out=ident[:], in_=ident[:], compare_op=ALU.not_equal, fill=1.0, base=0,
                                    pattern=[[-1, P]], channel_multiplier=1).then_inc(S["ident_ready"], 1)
            nc.gpsimd.memset(suffix[:], 0.0)
            pool.wait_ge(S["half_ready"], 1)
            normal_rstd(0)
            chain.step(nc.gpsimd.memset(causal[:], 1.0))
            chain.step(nc.gpsimd.affine_select(out=causal[:], in_=causal[:], compare_op=ALU.is_ge, fill=0.0, base=0,
                                               pattern=[[-1, P]], channel_multiplier=1))
            for m in range(1, NT):
                v = suffix[:, m, :].rearrange("p (t r) -> p t r", r=ROWS)
                chain.step(nc.gpsimd.memset(v[:, 0:m, E_ROW:E_ROW + 3], 1.0))
            chain.step(nc.gpsimd.memset(lhs_rows[:].bitcast(F32), 0.0))
            chain.step(nc.gpsimd.memset(rhs_rows[:].bitcast(F32), 0.0))
            chain.step(nc.gpsimd.iota(iota8[:], pattern=[[1, E]], base=0, channel_multiplier=0,
                                      allow_small_or_imprecise_dtypes=True))
            pool.sem_inc(S["consts_ready"], 1)
            pool.wait_ge(S["be_ready"], 1)

            def body(b):
                sum_experts(b, 0)
                sum_experts(b, 1)
                if not is_last(b):
                    normal_rstd(b + 1)
                sum_experts(b, 2)
                bias_rows(b)
                sum_experts(b, 3)
                bias_rhs(b)

            steady_chain(pool, body, chain)


_INS = ['L0_attn_x', 'L0_attn_Wq', 'L0_attn_Wk', 'L0_attn_Wv', 'L0_ffn_Wg', 'L0_ffn_We', 'L0_ffn_be']
_OUT = ((8, 512, 128), 'float32')


def kernel(**inputs):
    import numpy as _np
    import concourse.bacc as _bacc
    from concourse import mybir as _mybir
    from concourse.bass_utils import run_bass_kernel_spmd as _run

    nc = _bacc.Bacc("TRN2", target_bir_lowering=False, num_devices=1)
    arrays, args = {}, []
    for name in _INS:
        arrays[f"in_{name}_dram"] = _np.ascontiguousarray(inputs[name])
    r = _np.arange(P) % ROWS
    arrays["in_rows_dram"] = _np.where(((r >= 8) & (r < 16)) | (r == E_ROW + 1), -1.0, 0.0).astype(_np.float32)[:, None]
    arrays["in_pick_dram"] = ((r[None, :] % 8 == _np.arange(8)[:, None]) & (r[None, :] < E_ROW)).astype(_np.float32)
    for k, a in arrays.items():
        args.append(nc.dram_tensor(k, a.shape, _mybir.dt.from_np(a.dtype), kind="ExternalInput").ap())
    shape, dtype = _OUT
    o = nc.dram_tensor("out_0_dram", shape, _mybir.dt.from_np(_np.dtype(dtype)), kind="ExternalOutput").ap()
    build(nc, *args, o)
    return _run(nc, [arrays], core_ids=[0]).results[0]["out_0_dram"]
```

```python
from contextlib import ExitStack

import concourse.bass as bass
from concourse import mybir

F32 = mybir.dt.float32
F32R = mybir.dt.float32r
U32 = mybir.dt.uint32
ALU = mybir.AluOpType
ACT = mybir.ActivationFunctionType
AX_X = mybir.AxisListType.X

P = 128
EPS = 1e-5
GROUPS = "U C0 C1 C2 C3 SV B0 A0 A1 B1 A2 A3 B2 X B3 DT".split()
RING = 4
COLS = {"C": 2 * P + 8, "A": 4 * P, "B": 3 * P}
OFF = {"C": 0, "A": COLS["C"], "B": COLS["C"] + COLS["A"]}
Y_AT, G_AT = P, 2 * P
ROWS = 32
G_ROW = 3


class Chain:

    def __init__(self, engine, sem):
        self.engine, self.sem, self.n = engine, sem, 0

    def mark(self, instruction):
        self.n += 1
        instruction.then_inc(self.sem, 1)
        return self.n

    def need(self, count):
        self.engine.wait_ge(self.sem, count)

    def step(self, instruction):
        self.need(self.mark(instruction))


def build(nc, x, Wq, Wk, Wv, Wg, We, be, rows, pick, out):
    B, T, D = x.shape
    E = Wg.shape[1]
    NT = T // P
    assert D == P and NT == 4 and E == 8
    SCALE = float(T) ** -0.5
    NW = E * P + P + E

    x_v = x.rearrange("b (t p) d -> b p t d", p=P)
    out_v = out.rearrange("b (t p) d -> b p t d", p=P)

    with ExitStack() as ctx:
        def sb(name, shape, dt=F32):
            return ctx.enter_context(nc.sbuf_tensor(name, shape, dt))

        def ps(name):
            return ctx.enter_context(nc.psum_tensor(name, [P, 512], F32))

        def sem(name):
            return ctx.enter_context(nc.semaphore(name))

        wq_s, wk_s, wv_s = (sb(n, [P, P]) for n in ("wq_s", "wk_s", "wv_s"))
        w_f = sb("w_f", [P, NW])
        w_hi, w_lo = (sb(n, [P, NW], F32R) for n in ("w_hi", "w_lo"))
        a_hi, a_lo = (sb(n, [P, P], F32R) for n in ("a_hi", "a_lo"))
        be_s = sb("be_s", [E, P])
        rows_s = sb("rows_s", [P, 1])
        pick_s = sb("pick_s", [E, P])
        ident = sb("ident", [P, P])
        causal = sb("causal", [P, P])
        suffix = sb("suffix", [P, NT, P])
        iota8 = sb("iota8", [P, E])
        half = sb("half", [P, NT])
        ones = sb("ones", [P, NT, 2, E])
        x_all = sb("x_all", [P, B * NT * P])
        stats = sb("stats", [P, NT, 6])
        mv = sb("mv", [P, NT, 2])
        veps, rstd, nmean, nmr = (sb(n, [P, NT]) for n in ("veps", "rstd", "nmean", "nmr"))
        xn = sb("xn", [P, NT, P])
        xT_hi, xT_lo, uT_hi, uT_lo = (sb(n, [P, NT * P], F32R) for n in ("xT_hi", "xT_lo", "uT_hi", "uT_lo"))
        c_s = sb("c_s", [P, NT, COLS["C"]])
        prob = sb("prob", [P, 2, NT * P])
        probT = sb("probT", [P, NT, NT * P])
        mx, nmx, em, rs, tot, rinv, masked_keys = (sb(n, [P, NT]) for n in ("mx", "nmx", "em", "rs", "tot", "rinv", "masked_keys"))
        gate_tot = sb("gate_tot", [P, NT, E])
        top8 = sb("top8", [P, NT, E])
        below, gexp = (sb(n, [P, NT, E + 1]) for n in ("below", "gexp"))
        idx8 = sb("idx8", [P, NT, E], U32)
        chosen = sb("chosen", [P, NT, 2, E])
        picked, gnorm, gate = (sb(n, [P, NT, E]) for n in ("picked", "gnorm", "gate"))
        gsum, grec = (sb(n, [P, NT]) for n in ("gsum", "grec"))
        y7 = sb("y7", [P, NT, P])
        ysc = sb("ysc", [P, 2, 4, P])
        mix = sb("mix", [P, 2, 3, P])
        ffn = sb("ffn", [P, NT, P])
        lhs_rows = sb("lhs_rows", [P, NT * ROWS], F32R)
        lhsT_rows = sb("lhsT_rows", [P, P], F32R)
        sv_hi = sb("sv_hi", [P, P], F32R)
        rhs_rows = sb("rhs_rows", [P, NT, P], F32R)
        o_s = sb("o_s", [P, NT, P])

        ring = [ps(f"ring{i}") for i in range(RING)]
        score = [ps("score0"), ps("score1")]
        ptb = ps("ptb")
        attb = ps("attb")

        names = """w_att w_moe w_const x0 x1 x_rest a_done wvt_done a_ready w_ready wl_ready be_done be_ready
            wide_done scores_done pt_done pv_done xt_done sv_done dt_done u_done bias_done
            below_ready gexp_ready c_used a_used exp_done em_done pt_ready xn_ready xh_ready xl_ready uh_ready
            mix_ready ul_ready svh_ready dt_ready veps_ready nmean_ready rstd_ready stats_ready gate_ready nmx_ready
            tot_ready rinv_ready fin_done rows_ready ffn_ready y7_ready sv_rows_ready stored dve_chain
            act_chain pool_chain setup_hi half_ready ident_ready consts_ready"""
        S = {n: sem(n) for n in names.split()}

        block = ctx.enter_context(nc.Block())

        def tile_ap(b, t):
            return x_all[:, bass.ds(b * (NT * P) + t * P, P)]

        WIDE = [g for g in GROUPS if g[0] in "ABC"]

        def wide_count(k, b, t):
            return b * (3 * NT) + WIDE.index(f"{k}{t}") + 1

        def bank(g):
            return ring[GROUPS.index(g) % RING]

        def is_first(b):
            return b == 0

        def is_last(b):
            return b == B - 1

        @block.sync
        def _(sp):
            sp.dma_start(x_all[:, 0:NT * P].rearrange("p (t d) -> p t d", d=P), x_v[0]).then_inc(S["x0"], 16)
            sp.dma_start(wq_s[:], Wq).then_inc(S["w_att"], 16)
            sp.dma_start(wk_s[:], Wk).then_inc(S["w_att"], 16)
            sp.dma_start(w_f[:, OFF["A"]:OFF["A"] + 7 * P].rearrange("p (e h) -> p e h", h=P),
                         We[0:7].rearrange("e d h -> d e h")).then_inc(S["w_moe"], 16)
            sp.dma_start(x_all[:, NT * P:2 * NT * P].rearrange("p (t d) -> p t d", d=P), x_v[1]).then_inc(S["x1"], 16)
            for b in range(2, B):
                sp.dma_start(x_all[:, b * NT * P:(b + 1) * NT * P].rearrange("p (t d) -> p t d", d=P),
                             x_v[b]).then_inc(S["x_rest"], 16)

            def store(b):
                sp.wait_ge(S["fin_done"], b * NT + NT)
                sp.dma_start(out_v[b].rearrange("p t d -> p t d"), o_s[:, :, :]).then_inc(S["stored"], 16)

            for b in range(B):
                store(b)
            sp.wait_ge(S["stored"], 16 * B)

        @block.tensor
        def _(pe):
            def ring_free(g, b):
                n = GROUPS.index(g) - RING
                if n < 0 and is_first(b):
                    return
                if n < 0:
                    b = b - 1
                prev = GROUPS[n % len(GROUPS)]
                if prev == "X" and is_last(b):
                    return
                if prev == "X":
                    pe.wait_ge(S["xl_ready"], b + 2)
                elif prev in ("U", "SV", "DT"):
                    pe.wait_ge(S[{"U": "ul_ready", "SV": "sv_rows_ready", "DT": "dt_ready"}[prev]], b + 1)
                else:
                    pe.wait_ge(S[{"C": "c_used", "A": "a_used", "B": "mix_ready"}[prev[0]]], NT * b + int(prev[1]) + 1)

            def three(dst, hi, lo, w_h, w_l):
                nc.tensor.matmul(dst, hi, w_h, start=True, stop=False)
                nc.tensor.matmul(dst, hi, w_l, start=False, stop=False)
                return nc.tensor.matmul(dst, lo, w_h, start=False, stop=True)

            def wide(k, b, t):
                ring_free(f"{k}{t}", b)
                c = slice(OFF[k], OFF[k] + COLS[k])
                r = slice(t * P, (t + 1) * P)
                three(bank(f"{k}{t}")[:, 0:COLS[k]], xT_hi[:, r], xT_lo[:, r], w_hi[:, c], w_lo[:, c]
                      ).then_inc(S["wide_done"], 1)

            def scores(b, t):
                if t == 0:
                    pe.wait_ge(S["uh_ready"], b + 1)
                    pe.wait_ge(S["ul_ready"], b + 1)
                if not (is_first(b) and t < 2):
                    pe.wait_ge(S["exp_done"], b * NT + t - 1)
                r, n = slice(t * P, (t + 1) * P), (t + 1) * P
                three(score[t % 2][:, 0:n], uT_hi[:, r], uT_lo[:, r], xT_hi[:, 0:n], xT_lo[:, 0:n]
                      ).then_inc(S["scores_done"], 1)

            def transpose_probs(b, t):
                pe.wait_ge(S["exp_done"], b * NT + t + 1)
                if not (is_first(b) and t == 0):
                    pe.wait_ge(S["pt_ready"], b * NT + t)
                for j in range(t + 1):
                    last = nc.tensor.transpose(ptb[:, j * P:(j + 1) * P], prob[:, t % 2, j * P:(j + 1) * P], ident[:])
                last.then_inc(S["pt_done"], 1)

            def attend(b, t):
                pe.wait_ge(S["pt_ready"], b * NT + t + 1)
                if t == 0:
                    pe.wait_ge(S["c_used"], b * NT + NT)
                    if not is_first(b):
                        pe.wait_ge(S["fin_done"], b * NT)
                for j in range(t + 1):
                    last = nc.tensor.matmul(attb[:, t * P:(t + 1) * P], probT[:, t, j * P:(j + 1) * P],
                                            c_s[:, j, 0:P], start=(t == 0), stop=False, skip_group_check=True)
                last.then_inc(S["pv_done"], 1)

            def transpose_x(b, ready):
                pe.wait_ge(S["xn_ready"], ready)
                for t in range(NT):
                    last = nc.tensor.transpose(bank("X")[:, t * P:(t + 1) * P], xn[:, t, :], ident[:])
                last.then_inc(S["xt_done"], 1)

            def project_u(b):
                ring_free("U", b)
                pe.wait_ge(S["xh_ready"], b + 1)
                pe.wait_ge(S["xl_ready"], b + 1)
                dst = bank("U")[:, :]
                nc.tensor.matmul(dst, a_hi[:], xT_hi[:], start=True, stop=False)
                nc.tensor.matmul(dst, a_lo[:], xT_hi[:], start=False, stop=False)
                nc.tensor.matmul(dst, a_hi[:], xT_lo[:], start=False, stop=True).then_inc(S["u_done"], 1)

            def value_sums(b):
                ring_free("SV", b)
                pe.wait_ge(S["c_used"], b * NT + NT)
                for m in range(1, NT):
                    last = nc.tensor.matmul(bank("SV")[:, 0:P], suffix[:, m, :], c_s[:, m, 0:P],
                                            start=(m == 1), stop=(m == NT - 1))
                last.then_inc(S["sv_done"], 1)

            def transpose_rows(b):
                ring_free("DT", b)
                pe.wait_ge(S["rows_ready"], b + 1)
                nc.tensor.transpose(bank("DT")[:, 0:P], lhs_rows[:].bitcast(F32), ident[:]).then_inc(S["dt_done"], 1)

            def bias(b):
                pe.wait_ge(S["sv_rows_ready"], b + 1)
                pe.wait_ge(S["dt_ready"], b + 1)
                nc.tensor.matmul(attb[:], lhsT_rows[:], rhs_rows[:].rearrange("p t h -> p (t h)"),
                                 start=False, stop=True, skip_group_check=True).then_inc(S["bias_done"], 1)

            def next_x(b):
                ring_free("X", b)
                if not is_last(b):
                    transpose_x(b, b * NT + 2 * NT)

            pe.wait_ge(S["w_att"], 32)
            nc.tensor.matmul(score[0][:, 0:P], wq_s[:], wk_s[:], start=True, stop=True).then_inc(S["a_done"], 1)
            pe.wait_ge(S["ident_ready"], 1)
            transpose_x(0, NT)
            pe.wait_ge(S["w_const"], 64)
            nc.tensor.transpose(attb[:, 0:P], wv_s[:], ident[:]).then_inc(S["wvt_done"], 1)
            nc.tensor.matmul(ptb[:, 0:P], pick_s[:], be_s[:], start=True, stop=True).then_inc(S["be_done"], 1)
            pe.wait_ge(S["a_ready"], 1)

            def body(b):
                project_u(b)
                if is_first(b):
                    pe.wait_ge(S["wl_ready"], 1)
                wide("C", b, 0)
                wide("C", b, 1)
                wide("C", b, 2)
                wide("C", b, 3)
                scores(b, 0)
                scores(b, 1)
                value_sums(b)
                wide("B", b, 0)
                wide("A", b, 0)
                transpose_probs(b, 0)
                scores(b, 2)
                wide("A", b, 1)
                wide("B", b, 1)
                wide("A", b, 2)
                transpose_probs(b, 1)
                scores(b, 3)
                attend(b, 0)
                transpose_probs(b, 2)
                wide("A", b, 3)
                wide("B", b, 2)
                next_x(b)
                wide("B", b, 3)
                transpose_probs(b, 3)
                attend(b, 1)
                attend(b, 2)
                attend(b, 3)
                transpose_rows(b)
                bias(b)

            for b in range(B):
                body(b)

        @block.vector
        def _(dve):
            chain = Chain(dve, S["dve_chain"])

            def normal_stats(b, tiles):
                for t in tiles:
                    nc.vector.bn_stats(stats[:, t, :], tile_ap(b, t)).then_inc(S["stats_ready"], 1)

            def normal_finish(b):
                dve.wait_ge(S["stats_ready"], b * NT + NT)
                for t in range(NT):
                    last = nc.vector.bn_aggr(mv[:, t, :], stats[:, t, :])
                chain.step(last)
                if not is_first(b):
                    dve.wait_ge(S["rstd_ready"], b)
                nc.vector.tensor_scalar(nmean[:], mv[:, :, 0], -1.0, None, ALU.mult).then_inc(S["nmean_ready"], 1)
                nc.vector.tensor_scalar_add(veps[:], mv[:, :, 1], EPS).then_inc(S["veps_ready"], 1)

            def split_lo(dst, src, hi, done):
                nc.vector.tensor_tensor(dst, src, hi.bitcast(F32), ALU.subtract).then_inc(done, 1)

            cnt = {}

            def gate_max(b):
                dve.wait_ge(S["c_used"], b * NT + NT)
                for t in range(NT):
                    last = nc.vector.max(top8[:, t, :], c_s[:, t, G_AT:G_AT + E])
                cnt["top"] = chain.mark(last)

            def gate_below(b):
                chain.need(cnt["top"])
                if not is_first(b):
                    dve.wait_ge(S["gexp_ready"], b)
                top = top8[:, :, 0:1]
                nc.vector.tensor_tensor(below[:, :, E:E + 1], top8[:, :, 1:2], top, ALU.subtract)
                nc.vector.tensor_tensor(below[:, :, 0:E], c_s[:, :, G_AT:G_AT + E], top.to_broadcast([P, NT, E]),
                                        ALU.subtract).then_inc(S["below_ready"], 1)

            def gate_index(b):
                chain.need(cnt["top"])
                for t in range(NT):
                    last = nc.vector.max_index(idx8[:, t, :], top8[:, t, :], c_s[:, t, G_AT:G_AT + E])
                cnt["idx"] = chain.mark(last)

            def gate_chosen(b):
                chain.need(cnt["idx"])
                cnt["chosen"] = chain.mark(nc.vector.tensor_tensor(
                    chosen[:], iota8[:].unsqueeze(1).unsqueeze(1).to_broadcast([P, NT, 2, E]),
                    idx8[:, :, 0:2].unsqueeze(3).to_broadcast([P, NT, 2, E]), ALU.is_equal))

            def gate_picked(b):
                chain.need(cnt["chosen"])
                cnt["picked"] = chain.mark(nc.vector.tensor_tensor(picked[:], chosen[:, :, 0, :], chosen[:, :, 1, :],
                                                                   ALU.add))

            def gate_sum(b):
                dve.wait_ge(S["gexp_ready"], b + 1)
                cnt["gsum"] = chain.mark(nc.vector.tensor_scalar_add(gsum[:], gexp[:, :, E], 1.0))

            def gate_rec(b):
                chain.need(cnt["gsum"])
                cnt["grec"] = chain.mark(nc.vector.reciprocal(grec[:], gsum[:]))

            def gate_norm(b):
                chain.need(cnt["grec"])
                cnt["gnorm"] = chain.mark(nc.vector.tensor_tensor(
                    gnorm[:], gexp[:, :, 0:E], grec[:].unsqueeze(2).to_broadcast([P, NT, E]), ALU.mult))

            def gate_out(b):
                chain.need(max(cnt["gnorm"], cnt["picked"]))
                if not is_first(b):
                    dve.wait_ge(S["rows_ready"], b)
                    dve.wait_ge(S["a_used"], b * NT)
                    dve.wait_ge(S["mix_ready"], b * NT)
                nc.vector.tensor_tensor(gate[:], gnorm[:], picked[:], ALU.mult).then_inc(S["gate_ready"], 1)

            def mix_b(b, t, i):
                if i == 0:
                    dve.wait_ge(S["wide_done"], wide_count("B", b, t))
                    if t == 0:
                        dve.wait_ge(S["gate_ready"], b + 1)
                    if not (is_first(b) and t < 2):
                        dve.wait_ge(S["ffn_ready"], b * NT + t - 1)
                else:
                    chain.need(cnt[f"mix{t}{i - 1}"])
                before = tile_ap(b, t) if i == 0 else mix[:, t % 2, i - 1, :]
                ins = nc.vector.scalar_tensor_tensor(mix[:, t % 2, i, :], bank(f"B{t}")[:, i * P:(i + 1) * P],
                                                     gate[:, t, 4 + i:5 + i], before, ALU.mult, ALU.add)
                if i < 2:
                    cnt[f"mix{t}{i}"] = chain.mark(ins)
                else:
                    ins.then_inc(S["mix_ready"], 1)

            def mask_scores(b, t):
                dve.wait_ge(S["scores_done"], b * NT + t + 1)
                diag = score[t % 2][:, t * P:(t + 1) * P]
                cnt[f"masked{t}"] = chain.mark(nc.vector.tensor_tensor(diag, diag, causal[:], ALU.mult))

            def max_scores(b, t):
                chain.need(cnt[f"masked{t}"])
                cnt[f"maxed{t}"] = chain.mark(nc.vector.reduce_max(mx[:, t:t + 1], score[t % 2][:, 0:(t + 1) * P], AX_X))

            def negate_max(b, t):
                chain.need(cnt[f"maxed{t}"])
                if t == 0 and not is_first(b):
                    dve.wait_ge(S["exp_done"], b * NT)
                    dve.wait_ge(S["em_done"], b)
                if t < NT - 1:
                    ins = nc.vector.tensor_scalar(nmx[:, t:t + 1], mx[:, t:t + 1], -SCALE, 0.0, ALU.mult, ALU.min)
                else:
                    ins = nc.vector.tensor_scalar(nmx[:, t:t + 1], mx[:, t:t + 1], -SCALE, None, ALU.mult)
                ins.then_inc(S["nmx_ready"], 1)

            def softmax_sum(b):
                dve.wait_ge(S["exp_done"], b * NT + NT)
                dve.wait_ge(S["em_done"], b + 1)
                cnt["tot0"] = chain.mark(nc.vector.tensor_tensor(tot[:], em[:], masked_keys[:], ALU.mult))

            def softmax_tot(b):
                chain.need(cnt["tot0"])
                if not is_first(b):
                    dve.wait_ge(S["rows_ready"], b)
                nc.vector.tensor_tensor(tot[:], tot[:], rs[:], ALU.add).then_inc(S["tot_ready"], 1)

            def softmax_rec(b):
                dve.wait_ge(S["tot_ready"], b + 1)
                nc.vector.reciprocal(rinv[:], tot[:]).then_inc(S["rinv_ready"], 1)

            def finish_tile(b, t):
                if t == 0:
                    dve.wait_ge(S["bias_done"], b + 1)
                    dve.wait_ge(S["rinv_ready"], b + 1)
                    if not is_first(b):
                        dve.wait_ge(S["stored"], b * 16)
                dve.wait_ge(S["ffn_ready"], b * NT + t + 1)
                nc.vector.scalar_tensor_tensor(o_s[:, t, :], attb[:, t * P:(t + 1) * P], rinv[:, t:t + 1], ffn[:, t, :],
                                               ALU.mult, ALU.add).then_inc(S["fin_done"], 1)

            def sv_rows(b, t):
                if t == 0:
                    dve.wait_ge(S["svh_ready"], b + 1)
                    if not is_first(b):
                        dve.wait_ge(S["bias_done"], b)
                r = slice(t * ROWS, t * ROWS + G_ROW)
                ins = nc.vector.scalar_tensor_tensor(rhs_rows[r, t, :], sv_hi[r, :].bitcast(F32), rows_s[r, :],
                                                     bank("SV")[r, 0:P], ALU.mult, ALU.add)
                if t == NT - 2:
                    ins.then_inc(S["sv_rows_ready"], 1)

            def u_lo(b):
                dve.wait_ge(S["uh_ready"], b + 1)
                split_lo(uT_lo[:], bank("U")[:], uT_hi[:], S["ul_ready"])

            def x_lo(b):
                if not is_last(b):
                    dve.wait_ge(S["xh_ready"], b + 2)
                    split_lo(xT_lo[:], bank("X")[:], xT_hi[:], S["xl_ready"])

            def next_stats(b, t):
                if not is_last(b):
                    if t == 0:
                        dve.wait_ge(S["x1" if is_first(b) else "x_rest"], 16 if is_first(b) else 16 * (B - 2))
                    normal_stats(b + 1, (t,))

            def next_finish(b):
                if not is_last(b):
                    normal_finish(b + 1)

            dve.wait_ge(S["x0"], 16)
            normal_stats(0, range(NT))
            normal_finish(0)
            nc.vector.memset(half[:], -0.5).then_inc(S["half_ready"], 1)
            dve.wait_ge(S["xt_done"], 1)
            dve.wait_ge(S["xh_ready"], 1)
            split_lo(xT_lo[:], bank("X")[:], xT_hi[:], S["xl_ready"])
            dve.wait_ge(S["setup_hi"], 1)
            split_lo(a_lo[:], score[0][:, 0:P], a_hi[:], S["a_ready"])
            dve.wait_ge(S["setup_hi"], 2)
            dve.wait_ge(S["consts_ready"], 1)
            for t in range(NT):
                r = slice(t * ROWS, (t + 1) * ROWS)
                last = nc.vector.scalar_tensor_tensor(rhs_rows[r, t, :], sv_hi[r, :].bitcast(F32), rows_s[r, :],
                                                      ptb[r, 0:P], ALU.mult, ALU.add)
            last.then_inc(S["be_ready"], 1)
            dve.wait_ge(S["w_ready"], 1)
            split_lo(w_lo[:], w_f[:], w_hi[:], S["wl_ready"])

            def body(b):
                u_lo(b)
                next_stats(b, 0)
                gate_max(b)
                mask_scores(b, 0)
                gate_below(b)
                gate_index(b)
                max_scores(b, 0)
                gate_sum(b)
                gate_rec(b)
                gate_chosen(b)
                sv_rows(b, 0)
                gate_picked(b)
                gate_norm(b)
                negate_max(b, 0)
                mask_scores(b, 1)
                gate_out(b)
                sv_rows(b, 1)
                max_scores(b, 1)
                sv_rows(b, 2)
                mix_b(b, 0, 0)
                negate_max(b, 1)
                next_stats(b, 1)
                mix_b(b, 0, 1)
                mask_scores(b, 2)
                mix_b(b, 0, 2)
                next_stats(b, 2)
                max_scores(b, 2)
                mix_b(b, 1, 0)
                next_stats(b, 3)
                mix_b(b, 1, 1)
                negate_max(b, 2)
                next_finish(b)
                mask_scores(b, 3)
                mix_b(b, 1, 2)
                max_scores(b, 3)
                negate_max(b, 3)
                mix_b(b, 2, 0)
                mix_b(b, 2, 1)
                softmax_sum(b)
                mix_b(b, 2, 2)
                softmax_tot(b)
                mix_b(b, 3, 0)
                mix_b(b, 3, 1)
                x_lo(b)
                mix_b(b, 3, 2)
                softmax_rec(b)
                finish_tile(b, 0)
                finish_tile(b, 1)
                finish_tile(b, 2)
                finish_tile(b, 3)

            for b in range(B):
                body(b)

        @block.scalar
        def _(act):
            act.dma_start(wv_s[:], Wv).then_inc(S["w_const"], 16)
            act.dma_start(w_f[:, G_AT:G_AT + E], Wg).then_inc(S["w_moe"], 16)
            act.dma_start(w_f[:, Y_AT:Y_AT + P], We[7]).then_inc(S["w_moe"], 16)
            act.dma_start(be_s[:], be).then_inc(S["w_const"], 16)
            act.dma_start(rows_s[:], rows).then_inc(S["w_const"], 16)
            act.dma_start(pick_s[:], pick).then_inc(S["w_const"], 16)

            def normalize(b):
                act.wait_ge(S["rstd_ready"], b + 1)
                if not is_first(b):
                    act.wait_ge(S["xt_done"], b)
                for t in range(NT):
                    nc.scalar.activation(xn[:, t, :], tile_ap(b, t), ACT.Identity, bias=nmr[:, t:t + 1],
                                         scale=rstd[:, t:t + 1]).then_inc(S["xn_ready"], 1)

            def c_copy(b, t):
                act.wait_ge(S["wide_done"], wide_count("C", b, t))
                if t == 0 and not is_first(b):
                    act.wait_ge(S["pv_done"], b * NT)
                    act.wait_ge(S["y7_ready"], b)
                nc.scalar.copy(c_s[:, t, :], bank(f"C{t}")[:, 0:COLS["C"]]).then_inc(S["c_used"], 1)

            def gate_exp(b):
                act.wait_ge(S["below_ready"], b + 1)
                if not is_first(b):
                    act.wait_ge(S["gate_ready"], b)
                nc.scalar.activation(gexp[:], below[:], ACT.Exp).then_inc(S["gexp_ready"], 1)

            def scale_experts(b, t):
                if t == 0:
                    act.wait_ge(S["gate_ready"], b + 1)
                if not (is_first(b) and t < 2):
                    act.wait_ge(S["ffn_ready"], b * NT + t - 1)
                act.wait_ge(S["wide_done"], wide_count("A", b, t))
                for e in range(4):
                    last = nc.scalar.mul(ysc[:, t % 2, e, :], bank(f"A{t}")[:, e * P:(e + 1) * P], gate[:, t, e:e + 1])
                last.then_inc(S["a_used"], 1)

            def softmax_exp(b, t):
                act.wait_ge(S["nmx_ready"], b * NT + t + 1)
                if not (is_first(b) and t < 2):
                    act.wait_ge(S["pt_done"], b * NT + t - 1)
                if t == 0 and not is_first(b):
                    act.wait_ge(S["tot_ready"], b)
                n = (t + 1) * P
                nc.scalar.activation(prob[:, t % 2, 0:n], score[t % 2][:, 0:n], ACT.Exp, bias=nmx[:, t:t + 1],
                                     scale=SCALE, accum_out=rs[:, t:t + 1]).then_inc(S["exp_done"], 1)

            def masked_exp(b):
                act.wait_ge(S["nmx_ready"], b * NT + NT - 1)
                if not is_first(b):
                    act.wait_ge(S["rows_ready"], b)
                nc.scalar.activation(em[:, 0:NT - 1], nmx[:, 0:NT - 1], ACT.Exp).then_inc(S["em_done"], 1)

            def probs_copy(b, t):
                act.wait_ge(S["pt_done"], b * NT + t + 1)
                if t == 0 and not is_first(b):
                    act.wait_ge(S["pv_done"], b * NT)
                n = (t + 1) * P
                nc.scalar.copy(probT[:, t, 0:n], ptb[:, 0:n]).then_inc(S["pt_ready"], 1)

            normalize(0)
            act.wait_ge(S["a_done"], 1)
            nc.scalar.copy(a_hi[:], score[0][:, 0:P]).then_inc(S["setup_hi"], 1)
            act.wait_ge(S["xt_done"], 1)
            nc.scalar.copy(xT_hi[:], bank("X")[:]).then_inc(S["xh_ready"], 1)
            act.wait_ge(S["be_done"], 1)
            nc.scalar.copy(sv_hi[:], ptb[:, 0:P]).then_inc(S["setup_hi"], 1)
            act.wait_ge(S["wvt_done"], 1)
            nc.scalar.copy(w_f[:, 0:P], attb[:, 0:P]).then_inc(S["act_chain"], 1)
            act.wait_ge(S["act_chain"], 1)
            act.wait_ge(S["w_moe"], 48)
            nc.scalar.copy(w_hi[:], w_f[:]).then_inc(S["w_ready"], 1)

            def u_hi(b):
                act.wait_ge(S["u_done"], b + 1)
                nc.scalar.copy(uT_hi[:], bank("U")[:]).then_inc(S["uh_ready"], 1)

            def x_hi(b):
                if not is_last(b):
                    act.wait_ge(S["xt_done"], b + 2)
                    act.wait_ge(S["wide_done"], b * (3 * NT) + 3 * NT)
                    act.wait_ge(S["scores_done"], b * NT + NT)
                    nc.scalar.copy(xT_hi[:], bank("X")[:]).then_inc(S["xh_ready"], 1)

            def sv_high(b):
                act.wait_ge(S["sv_done"], b + 1)
                if not is_first(b):
                    act.wait_ge(S["sv_rows_ready"], b)
                nc.scalar.copy(sv_hi[:], bank("SV")[:, 0:P]).then_inc(S["svh_ready"], 1)

            def rows_copy(b):
                act.wait_ge(S["dt_done"], b + 1)
                if not is_first(b):
                    act.wait_ge(S["bias_done"], b)
                nc.scalar.copy(lhsT_rows[:], bank("DT")[:, 0:P]).then_inc(S["dt_ready"], 1)

            def next_normal(b):
                if not is_last(b):
                    normalize(b + 1)

            def body(b):
                u_hi(b)
                c_copy(b, 0)
                c_copy(b, 1)
                c_copy(b, 2)
                c_copy(b, 3)
                gate_exp(b)
                sv_high(b)
                softmax_exp(b, 0)
                scale_experts(b, 0)
                softmax_exp(b, 1)
                scale_experts(b, 1)
                probs_copy(b, 0)
                probs_copy(b, 1)
                softmax_exp(b, 2)
                scale_experts(b, 2)
                masked_exp(b)
                probs_copy(b, 2)
                next_normal(b)
                softmax_exp(b, 3)
                scale_experts(b, 3)
                probs_copy(b, 3)
                x_hi(b)
                rows_copy(b)

            for b in range(B):
                body(b)

        @block.gpsimd
        def _(pool):
            chain = Chain(pool, S["pool_chain"])

            def normal_rstd(b):
                pool.wait_ge(S["veps_ready"], b + 1)
                if not is_first(b):
                    pool.wait_ge(S["xn_ready"], b * NT)
                pool.wait_ge(S["nmean_ready"], b + 1)
                chain.step(nc.gpsimd.tensor_tensor(rstd[:], veps[:], half[:], ALU.pow))
                nc.gpsimd.tensor_tensor(nmr[:], nmean[:], rstd[:], ALU.mult).then_inc(S["rstd_ready"], 1)

            def scale_last(b):
                pool.wait_ge(S["gate_ready"], b + 1)
                nc.gpsimd.tensor_tensor(y7[:], c_s[:, :, Y_AT:Y_AT + P], gate[:, :, 7:8].to_broadcast([P, NT, P]),
                                        ALU.mult).then_inc(S["y7_ready"], 1)

            def sum_experts(b, t):
                y = ysc[:, t % 2, :, :]
                pool.wait_ge(S["a_used"], b * NT + t + 1)
                chain.step(nc.gpsimd.tensor_tensor(y[:, 0:2, :], y[:, 0:2, :], y[:, 2:4, :], ALU.add))
                chain.step(nc.gpsimd.tensor_tensor(y[:, 0, :], y[:, 0, :], y[:, 1, :], ALU.add))
                pool.wait_ge(S["y7_ready"], b + 1)
                chain.step(nc.gpsimd.tensor_tensor(y[:, 0, :], y[:, 0, :], y7[:, t, :], ALU.add))
                pool.wait_ge(S["mix_ready"], b * NT + t + 1)
                if not is_first(b):
                    pool.wait_ge(S["fin_done"], b * NT + t + 1 - NT)
                nc.gpsimd.tensor_tensor(ffn[:, t, :], y[:, 0, :], mix[:, t % 2, 2, :], ALU.add
                                        ).then_inc(S["ffn_ready"], 1)

            def bias_rows(b):
                rows3 = lhs_rows[:].rearrange("p (t r) -> p t r", r=ROWS)
                n = NT - 1
                pool.wait_ge(S["em_done"], b + 1)
                pool.wait_ge(S["gate_ready"], b + 1)
                pool.wait_ge(S["tot_ready"], b + 1)
                if not is_first(b):
                    pool.wait_ge(S["dt_done"], b)
                tot_g = chain.mark(nc.gpsimd.tensor_tensor(gate_tot[:], gate[:], tot[:].unsqueeze(2).to_broadcast(
                    [P, NT, E]), ALU.mult))
                e_hi = chain.mark(nc.gpsimd.tensor_tensor(rows3[:, 0:n, 0:2], em[:, 0:n].unsqueeze(2).to_broadcast(
                    [P, n, 2]), ones[:, 0:n, 0, 0:2], ALU.mult))
                chain.need(tot_g)
                g_hi = chain.mark(nc.gpsimd.tensor_tensor(
                    rows3[:, :, G_ROW:G_ROW + 2 * E].rearrange("p t (c e) -> p t c e", e=E),
                    gate_tot[:].unsqueeze(2).to_broadcast([P, NT, 2, E]), ones[:], ALU.mult))
                chain.need(e_hi)
                nc.gpsimd.tensor_tensor(rows3[:, 0:n, 2], em[:, 0:n], rows3[:, 0:n, 0].bitcast(F32), ALU.subtract)
                chain.need(g_hi)
                nc.gpsimd.tensor_tensor(rows3[:, :, G_ROW + 2 * E:G_ROW + 3 * E], gate_tot[:],
                                        rows3[:, :, G_ROW:G_ROW + E].bitcast(F32), ALU.subtract
                                        ).then_inc(S["rows_ready"], 1)

            chain.step(nc.gpsimd.memset(ones[:], 1.0))
            chain.step(nc.gpsimd.memset(ident[:], 0.0))
            nc.gpsimd.affine_select(out=ident[:], in_=ident[:], compare_op=ALU.not_equal, fill=1.0, base=0,
                                    pattern=[[-1, P]], channel_multiplier=1).then_inc(S["ident_ready"], 1)
            nc.gpsimd.memset(suffix[:], 0.0)
            pool.wait_ge(S["half_ready"], 1)
            normal_rstd(0)
            chain.step(nc.gpsimd.memset(causal[:], 1.0))
            chain.step(nc.gpsimd.affine_select(out=causal[:], in_=causal[:], compare_op=ALU.is_ge, fill=0.0, base=0,
                                               pattern=[[-1, P]], channel_multiplier=1))
            for m in range(1, NT):
                v = suffix[:, m, :].rearrange("p (t r) -> p t r", r=ROWS)
                chain.step(nc.gpsimd.memset(v[:, 0:m, 0:G_ROW], 1.0))
            chain.step(nc.gpsimd.memset(lhs_rows[:].bitcast(F32), 0.0))
            chain.step(nc.gpsimd.memset(rhs_rows[:].bitcast(F32), 0.0))
            chain.step(nc.gpsimd.iota(iota8[:], pattern=[[1, E]], base=0, channel_multiplier=0,
                                      allow_small_or_imprecise_dtypes=True))
            chain.step(nc.gpsimd.memset(em[:], 0.0))
            for t in range(NT):
                chain.step(nc.gpsimd.memset(masked_keys[:, t:t + 1], float(T - (t + 1) * P)))
            pool.sem_inc(S["consts_ready"], 1)

            def next_rstd(b):
                if not is_last(b):
                    normal_rstd(b + 1)

            def body(b):
                scale_last(b)
                sum_experts(b, 0)
                next_rstd(b)
                sum_experts(b, 1)
                sum_experts(b, 2)
                bias_rows(b)
                sum_experts(b, 3)

            for b in range(B):
                body(b)


_INS = ['L0_attn_x', 'L0_attn_Wq', 'L0_attn_Wk', 'L0_attn_Wv', 'L0_ffn_Wg', 'L0_ffn_We', 'L0_ffn_be']
_OUT = ((8, 512, 128), 'float32')


def kernel(**inputs):
    import numpy as _np
    import concourse.bacc as _bacc
    from concourse import mybir as _mybir
    from concourse.bass_utils import run_bass_kernel_spmd as _run

    nc = _bacc.Bacc("TRN2", target_bir_lowering=False, num_devices=1)
    arrays, args = {}, []
    for name in _INS:
        arrays[f"in_{name}_dram"] = _np.ascontiguousarray(inputs[name])
    r = _np.arange(P) % ROWS
    arrays["in_rows_dram"] = _np.where(((r >= G_ROW + 8) & (r < G_ROW + 16)) | (r == 1), -1.0, 0.0).astype(_np.float32)[:, None]
    arrays["in_pick_dram"] = (((r - G_ROW)[None, :] % 8 == _np.arange(8)[:, None]) & (r >= G_ROW) & (r < G_ROW + 24)).astype(_np.float32)
    for k, a in arrays.items():
        args.append(nc.dram_tensor(k, a.shape, _mybir.dt.from_np(a.dtype), kind="ExternalInput").ap())
    shape, dtype = _OUT
    o = nc.dram_tensor("out_0_dram", shape, _mybir.dt.from_np(_np.dtype(dtype)), kind="ExternalOutput").ap()
    build(nc, *args, o)
    return _run(nc, [arrays], core_ids=[0]).results[0]["out_0_dram"]
```

```python
from contextlib import ExitStack

import concourse.bass as bass
from concourse import mybir

F32 = mybir.dt.float32
F32R = mybir.dt.float32r
U32 = mybir.dt.uint32
ALU = mybir.AluOpType
ACT = mybir.ActivationFunctionType
AX_X = mybir.AxisListType.X

P = 128
EPS = 1e-5
RING = 4
SCORE_BANKS = 3
WARM = (5, 5)
COLS = {"C": 2 * P + 8, "A": 4 * P, "B": 3 * P}
OFF = {"C": 0, "A": COLS["C"], "B": COLS["C"] + COLS["A"]}
Y_AT, G_AT = P, 2 * P
FIRST_GROUPS = """C0@0 U@0 C1@0 C2@0 C3@0 SV@0 A0@0 B0@0 X@1 A1@0 B1@0 C0@1 U@1 C1@1 C2@1 A2@0""".split()
GROUPS = "C3 B2- B3- A3- SV DT- A0 B0 X+ A1 B1 C0+ U+ C1+ C2+ A2".split()
LAST_GROUPS = """B2@-2 C3@-1 B3@-2 A3@-2 SV@-1 DT@-2 A0@-1 B0@-1 A1@-1 B1@-1 A2@-1 B2@-1 B3@-1 A3@-1 DT@-1""".split()
ROWS = 32
G_ROW = 3


class Chain:

    def __init__(self, engine, sem):
        self.engine, self.sem, self.n = engine, sem, 0

    def mark(self, instruction):
        self.n += 1
        instruction.then_inc(self.sem, 1)
        return self.n

    def need(self, count):
        self.engine.wait_ge(self.sem, count)

    def step(self, instruction):
        self.need(self.mark(instruction))


def build(nc, x, w_attention, w_stacked, be, shapes, out):
    B, T, D = x.shape
    E = be.shape[0]
    NT = T // P
    assert D == P and NT == 4 and E == 8
    SCALE = float(T) ** -0.5
    NW = E * P + P + E

    x_v = x.rearrange("b (t p) d -> b p t d", p=P)
    out_v = out.rearrange("b (t p) d -> b p t d", p=P)

    with ExitStack() as ctx:
        def sb(name, shape, dt=F32):
            return ctx.enter_context(nc.sbuf_tensor(name, shape, dt))

        def ps(name):
            return ctx.enter_context(nc.psum_tensor(name, [P, 512], F32))

        def sem(name):
            return ctx.enter_context(nc.semaphore(name))

        wqk_s = sb("wqk_s", [P, 2 * P])
        w_f = sb("w_f", [P, NW])
        w_hi, w_lo = (sb(n, [P, NW], F32R) for n in ("w_hi", "w_lo"))
        a_hi, a_lo = (sb(n, [P, P], F32R) for n in ("a_hi", "a_lo"))
        be_s = sb("be_s", [E, P])
        shapes_s = sb("shapes_s", [P, P + 1])
        warm = sb("warm", [P, 1])
        ident = sb("ident", [P, P])
        causal = sb("causal", [P, NT * P])
        suffix = sb("suffix", [P, NT, P])
        iota8 = sb("iota8", [P, E])
        half = sb("half", [P, NT])
        ones = sb("ones", [P, NT, 2, E])
        x_all = sb("x_all", [P, B * NT * P])
        stats = sb("stats", [P, NT, 6])
        mv = sb("mv", [P, NT, 2])
        veps, rstd, nmean, nmr = (sb(n, [P, NT]) for n in ("veps", "rstd", "nmean", "nmr"))
        xn = sb("xn", [P, NT, P])
        xT_hi, xT_lo, uT_hi, uT_lo = (sb(n, [P, 2, NT * P], F32R) for n in ("xT_hi", "xT_lo", "uT_hi", "uT_lo"))
        c_s = sb("c_s", [P, 2, NT, COLS["C"]])
        prob = sb("prob", [P, NT, NT * P])
        probT = sb("probT", [P, 2, NT, NT * P])
        mx, nmx, em, rs, tot, rinv = (sb(n, [P, 2, NT]) for n in ("mx", "nmx", "em", "rs", "tot", "rinv"))
        masked_keys = sb("masked_keys", [P, NT])
        gate_tot = sb("gate_tot", [P, NT, E])
        top8 = sb("top8", [P, NT, E])
        below, gexp = (sb(n, [P, NT, E + 1]) for n in ("below", "gexp"))
        idx8 = sb("idx8", [P, NT, E], U32)
        chosen = sb("chosen", [P, NT, 2, E])
        picked, gnorm = (sb(n, [P, NT, E]) for n in ("picked", "gnorm"))
        gate = sb("gate", [P, 2, NT, E])
        gsum, grec = (sb(n, [P, NT]) for n in ("gsum", "grec"))
        y7 = sb("y7", [P, 2, NT, P])
        ysc = sb("ysc", [P, NT, 4, P])
        mix = sb("mix", [P, NT, 3, P])
        ffn = sb("ffn", [P, 2, NT, P])
        lhs_rows = sb("lhs_rows", [P, NT * ROWS], F32R)
        lhsT_rows = sb("lhsT_rows", [P, P], F32R)
        sv_hi = sb("sv_hi", [P, P], F32R)
        rhs_rows = sb("rhs_rows", [P, NT, P], F32R)
        o_s = sb("o_s", [P, 2, NT, P])

        ring = [ps(f"ring{i}") for i in range(RING)]
        score = [ps(f"score{i}") for i in range(SCORE_BANKS)]
        attb = ps("attb")

        names = """w_att w_moe w_const x0 x1 x_rest a_done a_ready be_done be_ready wide_done scores_done pt_done
            pv_done xt_done sv_done dt_done u_done bias_done below_ready gexp_ready c_used a_used exp_done
            em_done pt_ready xn_ready xh_ready xl_ready uh_ready mix_ready ul_ready svh_ready dt_ready
            veps_ready nmean_ready rstd_ready stats_ready gate_ready nmx_ready tot_ready rinv_ready fin_done
            rows_ready ffn_ready y7_ready sv_rows_ready stored0 stored_last ones_ready xn0_dve_ready
            wc_ready wcl_ready xt_late_done xh_late_ready rstd0_ready wa_ready wb_ready wla_ready wlb_ready
            ah_ready beh_ready stored1 dve_chain pool_chain ident_ready consts_ready"""
        S = {n: sem(n) for n in names.split()}

        block = ctx.enter_context(nc.Block())

        def tile_ap(b, t):
            return x_all[:, bass.ds(b * (NT * P) + t * P, P)]

        sequence = [("X", 0)]
        for g in FIRST_GROUPS:
            sequence.append((g.split("@")[0], int(g.split("@")[1])))
        for n in range(1, B - 1):
            for g in GROUPS:
                sequence.append((g.rstrip("+-"), n + g.count("+") - g.count("-")))
        for g in LAST_GROUPS:
            sequence.append((g.split("@")[0], B + int(g.split("@")[1])))
        place = {g: i for i, g in enumerate(sequence)}
        wide_place = {g: i for i, g in enumerate([g for g in sequence if g[0][0] in "ABC"])}

        def wide_count(k, b, t):
            return wide_place[f"{k}{t}", b] + 1

        c_cols, a_cols, b_cols = (slice(OFF[k], OFF[k] + COLS[k]) for k in "CAB")

        def score_bank(b, t):
            return score[(b * NT + t) % SCORE_BANKS]

        late_x = score[2]

        def bank(g, b):
            return ring[place[g, b] % RING]

        @block.sync
        def _(sp):
            sp.dma_start(x_all[:, 0:NT * P].rearrange("p (t d) -> p t d", d=P), x_v[0]).then_inc(S["x0"], 16)
            sp.dma_start(w_f[:], w_stacked).then_inc(S["w_moe"], 16)
            sp.dma_start(x_all[:, NT * P:2 * NT * P].rearrange("p (t d) -> p t d", d=P), x_v[1]).then_inc(S["x1"], 16)
            for b in range(2, B):
                sp.dma_start(x_all[:, b * NT * P:(b + 1) * NT * P].rearrange("p (t d) -> p t d", d=P),
                             x_v[b]).then_inc(S["x_rest"], 16)

            def store(b):
                sp.wait_ge(S["fin_done"], b * NT + NT)
                sp.dma_start(out_v[b], o_s[:, b % 2, :, :]).then_inc(S[f"stored{b % 2}"], 16)

            for b in range(B - 1):
                store(b)
            b, t = B - 1, NT - 1
            sp.wait_ge(S["fin_done"], b * NT + t)
            sp.dma_start(out_v[b][:, 0:t, :], o_s[:, b % 2, 0:t, :]).then_inc(S[f"stored{b % 2}"], 16)
            sp.wait_ge(S["fin_done"], b * NT + NT)
            sp.dma_start(out_v[b][:, t, :], o_s[:, b % 2, t, :]).then_inc(S["stored_last"], 16)
            sp.wait_ge(S["stored_last"], 16)
            for i in range(2):
                sp.wait_ge(S[f"stored{i}"], 16 * (B // 2))

        @block.tensor
        def _(pe):
            def ring_free(g, b):
                n = place[g, b] - RING
                if n < 0:
                    return
                prev, b = sequence[n]
                if prev == "X":
                    pe.wait_ge(S["xl_ready"], b + 1)
                elif prev in ("U", "SV", "DT"):
                    pe.wait_ge(S[{"U": "ul_ready", "SV": "sv_rows_ready", "DT": "dt_ready"}[prev]], b + 1)
                else:
                    pe.wait_ge(S[{"C": "c_used", "A": "a_used", "B": "mix_ready"}[prev[0]]], NT * b + int(prev[1]) + 1)

            def three(dst, hi, lo, w_h, w_l, lo_ready=None):
                nc.tensor.matmul(dst, hi, w_h, start=True, stop=False)
                nc.tensor.matmul(dst, hi, w_l, start=False, stop=False)
                if lo_ready:
                    pe.wait_ge(*lo_ready)
                return nc.tensor.matmul(dst, lo, w_h, start=False, stop=True)

            def wide(b, k, t):
                ring_free(f"{k}{t}", b)
                if t == 0 and k == "C":
                    pe.wait_ge(S["xh_ready"], b + 1)
                    if b == 0:
                        pe.wait_ge(S["wcl_ready"], 1)
                if t == 0 and k in "AB" and b == 0:
                    pe.wait_ge(S["wla_ready" if k == "A" else "wlb_ready"], 1)
                c = slice(OFF[k], OFF[k] + COLS[k])
                r = slice(t * P, (t + 1) * P)
                three(bank(f"{k}{t}", b)[:, 0:COLS[k]], xT_hi[:, b % 2, r], xT_lo[:, b % 2, r], w_hi[:, c], w_lo[:, c],
                      (S["xl_ready"], b + 1) if t == 0 and k == "C" else None).then_inc(S["wide_done"], 1)

            def scores(b, t):
                if t == 0:
                    pe.wait_ge(S["uh_ready"], b + 1)
                if b * NT + t >= SCORE_BANKS:
                    pe.wait_ge(S["pt_ready"], b * NT + t + 1 - SCORE_BANKS)
                r, n = slice(t * P, (t + 1) * P), (t + 1) * P
                three(score_bank(b, t)[:, 0:n], uT_hi[:, b % 2, r], uT_lo[:, b % 2, r], xT_hi[:, b % 2, 0:n],
                      xT_lo[:, b % 2, 0:n], (S["ul_ready"], b + 1) if t == 0 else None).then_inc(S["scores_done"], 1)

            def transpose_probs(b, t):
                pe.wait_ge(S["exp_done"], b * NT + t + 1)
                for j in range(t + 1):
                    c = slice(j * P, (j + 1) * P)
                    last = nc.tensor.transpose(score_bank(b, t)[:, c], prob[:, t, c], ident[:])
                last.then_inc(S["pt_done"], 1)

            def attend(b, t):
                pe.wait_ge(S["pt_ready"], b * NT + t + 1)
                if t == 0:
                    pe.wait_ge(S["c_used"], b * NT + NT)
                    if b == 0:
                        pe.wait_ge(S["be_ready"], 1)
                    if b > 0:
                        pe.wait_ge(S["fin_done"], b * NT)
                for j in range(t + 1):
                    last = nc.tensor.matmul(attb[:, t * P:(t + 1) * P], probT[:, b % 2, t, j * P:(j + 1) * P],
                                            c_s[:, b % 2, j, 0:P], start=(t == 0), stop=False, skip_group_check=True)
                last.then_inc(S["pv_done"], 1)

            def transpose_x(b):
                ring_free("X", b)
                pe.wait_ge(S["xn_ready"], b + 1)
                for t in range(NT):
                    last = nc.tensor.transpose(bank("X", b)[:, t * P:(t + 1) * P], xn[:, t, :], ident[:])
                last.then_inc(S["xt_done"], 1)

            def project_u(b):
                ring_free("U", b)
                pe.wait_ge(S["xh_ready"], b + 1)
                dst = bank("U", b)[:, :]
                nc.tensor.matmul(dst, a_hi[:], xT_hi[:, b % 2, :], start=True, stop=False)
                nc.tensor.matmul(dst, a_lo[:], xT_hi[:, b % 2, :], start=False, stop=False)
                pe.wait_ge(S["xl_ready"], b + 1)
                nc.tensor.matmul(dst, a_hi[:], xT_lo[:, b % 2, :], start=False, stop=True).then_inc(S["u_done"], 1)

            def value_sums(b):
                ring_free("SV", b)
                pe.wait_ge(S["c_used"], b * NT + NT)
                for m in range(1, NT):
                    last = nc.tensor.matmul(bank("SV", b)[:, 0:P], suffix[:, m, :], c_s[:, b % 2, m, 0:P],
                                            start=(m == 1), stop=(m == NT - 1))
                last.then_inc(S["sv_done"], 1)

            def transpose_rows(b):
                ring_free("DT", b)
                pe.wait_ge(S["rows_ready"], b + 1)
                nc.tensor.transpose(bank("DT", b)[:, 0:P], lhs_rows[:].bitcast(F32), ident[:]).then_inc(S["dt_done"], 1)

            def bias(b):
                pe.wait_ge(S["sv_rows_ready"], b + 1)
                pe.wait_ge(S["dt_ready"], b + 1)
                nc.tensor.matmul(attb[:], lhsT_rows[:], rhs_rows[:].rearrange("p t h -> p (t h)"),
                                 start=False, stop=True, skip_group_check=True).then_inc(S["bias_done"], 1)

            def keep_warm(count):
                for _ in range(count):
                    nc.tensor.matmul(score[1][:, 0:P], ident[:], ident[:], start=True, stop=True)

            def expert_biases(b):
                pe.wait_ge(S["w_const"], 32)
                nc.tensor.matmul(attb[:, 0:P], shapes_s[0:E, 0:P], be_s[:], start=True, stop=True).then_inc(S["be_done"], 1)

            pe.wait_ge(S["ident_ready"], 1)
            keep_warm(WARM[0])
            pe.wait_ge(S["w_att"], 16)
            nc.tensor.matmul(score[0][:, 0:P], wqk_s[:, 0:P], wqk_s[:, P:2 * P], start=True, stop=True).then_inc(S["a_done"], 1)
            keep_warm(WARM[1])
            for t in (2, 3, 0, 1):
                done, count = [("xn_ready", 1), ("xn0_dve_ready", 3), ("xn0_dve_ready", 1), ("xn0_dve_ready", 2)][t]
                pe.wait_ge(S[done], count)
                last = nc.tensor.transpose((bank("X", 0) if t < 2 else late_x)[:, (t % 2) * P:(t % 2 + 1) * P], xn[:, t, :],
                                           ident[:])
                if t in (1, 3):
                    last.then_inc(S["xt_done" if t == 1 else "xt_late_done"], 1)
            pe.wait_ge(S["a_ready"], 1)

            expert_biases(0)
            wide(0, "C", 0)
            project_u(0)
            wide(0, "C", 1)
            wide(0, "C", 2)
            wide(0, "C", 3)
            scores(0, 0)
            value_sums(0)
            transpose_probs(0, 0)
            scores(0, 1)
            scores(0, 2)
            wide(0, "A", 0)
            wide(0, "B", 0)
            attend(0, 0)
            transpose_x(1)
            wide(0, "A", 1)
            scores(0, 3)
            wide(0, "B", 1)
            wide(1, "C", 0)
            project_u(1)
            transpose_probs(0, 1)
            wide(1, "C", 1)
            wide(1, "C", 2)
            wide(0, "A", 2)
            for n in range(1, B - 1):
                wide(n, "C", 3)
                wide(n - 1, "B", 2)
                wide(n - 1, "B", 3)
                attend(n - 1, 1)
                scores(n, 0)
                transpose_probs(n - 1, 2)
                wide(n - 1, "A", 3)
                transpose_probs(n - 1, 3)
                value_sums(n)
                attend(n - 1, 2)
                scores(n, 1)
                transpose_rows(n - 1)
                attend(n - 1, 3)
                bias(n - 1)
                wide(n, "A", 0)
                wide(n, "B", 0)
                scores(n, 2)
                transpose_x(n + 1)
                transpose_probs(n, 0)
                wide(n, "A", 1)
                wide(n, "B", 1)
                attend(n, 0)
                transpose_probs(n, 1)
                wide(n + 1, "C", 0)
                project_u(n + 1)
                scores(n, 3)
                wide(n + 1, "C", 1)
                wide(n + 1, "C", 2)
                wide(n, "A", 2)
            wide(B - 2, "B", 2)
            wide(B - 1, "C", 3)
            wide(B - 2, "B", 3)
            attend(B - 2, 1)
            transpose_probs(B - 2, 2)
            wide(B - 2, "A", 3)
            scores(B - 1, 0)
            transpose_probs(B - 2, 3)
            scores(B - 1, 1)
            value_sums(B - 1)
            attend(B - 2, 2)
            transpose_rows(B - 2)
            attend(B - 2, 3)
            bias(B - 2)
            wide(B - 1, "A", 0)
            transpose_probs(B - 1, 0)
            wide(B - 1, "B", 0)
            scores(B - 1, 2)
            wide(B - 1, "A", 1)
            wide(B - 1, "B", 1)
            scores(B - 1, 3)
            wide(B - 1, "A", 2)
            wide(B - 1, "B", 2)
            wide(B - 1, "B", 3)
            transpose_probs(B - 1, 1)
            wide(B - 1, "A", 3)
            attend(B - 1, 0)
            transpose_probs(B - 1, 2)
            transpose_probs(B - 1, 3)
            attend(B - 1, 1)
            attend(B - 1, 2)
            attend(B - 1, 3)
            transpose_rows(B - 1)
            bias(B - 1)

        @block.vector
        def _(dve):
            chain = Chain(dve, S["dve_chain"])

            def normal_stats(b, t):
                if t == 0 and b > 0:
                    dve.wait_ge(S["x1" if b == 1 else "x_rest"], 16 if b == 1 else 16 * (B - 2))
                nc.vector.bn_stats(stats[:, t, :], tile_ap(b, t)).then_inc(S["stats_ready"], 1)

            def normal_finish(b):
                dve.wait_ge(S["stats_ready"], b * NT + NT)
                for t in range(NT):
                    last = nc.vector.bn_aggr(mv[:, t, :], stats[:, t, :])
                chain.step(last)
                if b > 0:
                    dve.wait_ge(S["rstd_ready"], b)
                nc.vector.tensor_scalar_add(veps[:], mv[:, :, 1], EPS).then_inc(S["veps_ready"], 1)
                nc.vector.tensor_scalar(nmean[:], mv[:, :, 0], -1.0, None, ALU.mult).then_inc(S["nmean_ready"], 1)

            def split_lo(dst, src, hi, done):
                nc.vector.tensor_tensor(dst, src, hi.bitcast(F32), ALU.subtract).then_inc(done, 1)

            cnt = {}

            def gate_max(b):
                dve.wait_ge(S["c_used"], b * NT + NT)
                for t in range(NT):
                    last = nc.vector.max(top8[:, t, :], c_s[:, b % 2, t, G_AT:G_AT + E])
                cnt["top", b] = chain.mark(last)

            def gate_below(b):
                chain.need(cnt["top", b])
                if b > 0:
                    dve.wait_ge(S["gexp_ready"], b)
                top = top8[:, :, 0:1]
                nc.vector.tensor_tensor(below[:, :, E:E + 1], top8[:, :, 1:2], top, ALU.subtract)
                nc.vector.tensor_tensor(below[:, :, 0:E], c_s[:, b % 2, :, G_AT:G_AT + E], top.to_broadcast([P, NT, E]),
                                        ALU.subtract).then_inc(S["below_ready"], 1)

            def gate_index(b):
                chain.need(cnt["top", b])
                for t in range(NT):
                    last = nc.vector.max_index(idx8[:, t, :], top8[:, t, :], c_s[:, b % 2, t, G_AT:G_AT + E])
                cnt["idx", b] = chain.mark(last)

            def gate_chosen(b):
                chain.need(cnt["idx", b])
                cnt["chosen", b] = chain.mark(nc.vector.tensor_tensor(
                    chosen[:], iota8[:].unsqueeze(1).unsqueeze(1).to_broadcast([P, NT, 2, E]),
                    idx8[:, :, 0:2].unsqueeze(3).to_broadcast([P, NT, 2, E]), ALU.is_equal))

            def gate_picked(b):
                chain.need(cnt["chosen", b])
                cnt["picked", b] = chain.mark(nc.vector.tensor_tensor(picked[:], chosen[:, :, 0, :], chosen[:, :, 1, :],
                                                                   ALU.add))

            def gate_sum(b):
                dve.wait_ge(S["gexp_ready"], b + 1)
                cnt["gsum", b] = chain.mark(nc.vector.tensor_scalar_add(gsum[:], gexp[:, :, E], 1.0))

            def gate_rec(b):
                chain.need(cnt["gsum", b])
                cnt["grec", b] = chain.mark(nc.vector.reciprocal(grec[:], gsum[:]))

            def gate_norm(b):
                chain.need(cnt["grec", b])
                cnt["gnorm", b] = chain.mark(nc.vector.tensor_tensor(
                    gnorm[:], gexp[:, :, 0:E], grec[:].unsqueeze(2).to_broadcast([P, NT, E]), ALU.mult))

            def gate_out(b):
                chain.need(max(cnt["gnorm", b], cnt["picked", b]))
                if b > 1:
                    dve.wait_ge(S["rows_ready"], b - 1)
                    dve.wait_ge(S["a_used"], (b - 1) * NT)
                    dve.wait_ge(S["mix_ready"], (b - 1) * NT)
                    dve.wait_ge(S["y7_ready"], b - 1)
                nc.vector.tensor_tensor(gate[:, b % 2, :, :], gnorm[:], picked[:], ALU.mult).then_inc(S["gate_ready"], 1)

            def mix_b(b, t, i):
                if i == 0:
                    dve.wait_ge(S["wide_done"], wide_count("B", b, t))
                    if t == 0:
                        dve.wait_ge(S["gate_ready"], b + 1)
                    if b > 0:
                        dve.wait_ge(S["ffn_ready"], (b - 1) * NT + t + 1)
                else:
                    chain.need(cnt["mix", b, t, i - 1])
                before = tile_ap(b, t) if i == 0 else mix[:, t, i - 1, :]
                ins = nc.vector.scalar_tensor_tensor(mix[:, t, i, :], bank(f"B{t}", b)[:, i * P:(i + 1) * P],
                                                     gate[:, b % 2, t, 4 + i:5 + i], before, ALU.mult, ALU.add)
                if i < 2:
                    cnt["mix", b, t, i] = chain.mark(ins)
                else:
                    ins.then_inc(S["mix_ready"], 1)

            def mask_scores(b, t):
                dve.wait_ge(S["scores_done"], b * NT + t + 1)
                if t == 0 and b > 1:
                    dve.wait_ge(S["exp_done"], (b - 1) * NT)
                    dve.wait_ge(S["em_done"], b - 1)
                n = (t + 1) * P
                cnt["maxed", b, t] = chain.mark(nc.vector.tensor_tensor_reduce(
                    score_bank(b, t)[:, 0:n], score_bank(b, t)[:, 0:n], causal[:, (NT - 1 - t) * P:], SCALE,
                    0.0 if t < NT - 1 else -3e38, ALU.mult, ALU.max, accum_out=mx[:, b % 2, t:t + 1]))

            def negate_max(b, t):
                chain.need(cnt["maxed", b, t])
                nc.vector.tensor_scalar(nmx[:, b % 2, t:t + 1], mx[:, b % 2, t:t + 1], -1.0, None, ALU.mult
                                        ).then_inc(S["nmx_ready"], 1)

            def softmax_sum(b):
                dve.wait_ge(S["exp_done"], b * NT + NT)
                dve.wait_ge(S["em_done"], b + 1)
                if b > 1:
                    dve.wait_ge(S["rows_ready"], b - 1)
                cnt["tot0", b] = chain.mark(nc.vector.tensor_tensor(tot[:, b % 2, :], em[:, b % 2, :], masked_keys[:],
                                                                    ALU.mult))

            def softmax_tot(b):
                chain.need(cnt["tot0", b])
                nc.vector.tensor_tensor(tot[:, b % 2, :], tot[:, b % 2, :], rs[:, b % 2, :], ALU.add).then_inc(S["tot_ready"], 1)

            def softmax_rec(b):
                dve.wait_ge(S["tot_ready"], b + 1)
                nc.vector.reciprocal(rinv[:, b % 2, :], tot[:, b % 2, :]).then_inc(S["rinv_ready"], 1)

            def finish_tile(b, t):
                if t == 0:
                    dve.wait_ge(S["bias_done"], b + 1)
                    dve.wait_ge(S["rinv_ready"], b + 1)
                    if b > 1:
                        dve.wait_ge(S[f"stored{b % 2}"], b // 2 * 16)
                dve.wait_ge(S["ffn_ready"], b * NT + t + 1)
                nc.vector.scalar_tensor_tensor(o_s[:, b % 2, t, :], attb[:, t * P:(t + 1) * P], rinv[:, b % 2, t:t + 1],
                                               ffn[:, b % 2, t, :], ALU.mult, ALU.add).then_inc(S["fin_done"], 1)

            def sv_rows(b, t):
                if t == 0:
                    dve.wait_ge(S["svh_ready"], b + 1)
                    if b > 0:
                        dve.wait_ge(S["bias_done"], b)
                r = slice(t * ROWS, t * ROWS + G_ROW)
                ins = nc.vector.scalar_tensor_tensor(rhs_rows[r, t, :], sv_hi[r, :].bitcast(F32), shapes_s[r, P:P + 1],
                                                     bank("SV", b)[r, 0:P], ALU.mult, ALU.add)
                if t == NT - 2:
                    ins.then_inc(S["sv_rows_ready"], 1)

            def u_lo(b):
                dve.wait_ge(S["uh_ready"], b + 1)
                split_lo(uT_lo[:, b % 2, :], bank("U", b)[:], uT_hi[:, b % 2, :], S["ul_ready"])

            def x_lo(b):
                dve.wait_ge(S["xh_ready"], b + 1)
                split_lo(xT_lo[:, b % 2, :], bank("X", b)[:], xT_hi[:, b % 2, :], S["xl_ready"])

            def weights_lo(b):
                dve.wait_ge(S["wa_ready"], 1)
                split_lo(w_lo[:, a_cols], w_f[:, a_cols], w_hi[:, a_cols], S["wla_ready"])

            def bias_rhs(b):
                dve.wait_ge(S["beh_ready"], 1)
                dve.wait_ge(S["consts_ready"], 1)
                for t in range(NT):
                    r = slice(t * ROWS, (t + 1) * ROWS)
                    last = nc.vector.scalar_tensor_tensor(rhs_rows[r, t, :], sv_hi[r, :].bitcast(F32),
                                                          shapes_s[r, P:P + 1], attb[r, 0:P], ALU.mult, ALU.add)
                last.then_inc(S["be_ready"], 1)

            dve.wait_ge(S["x0"], 16)
            for t in range(NT):
                normal_stats(0, t)
            normal_finish(0)
            dve.wait_ge(S["wc_ready"], 1)
            split_lo(w_lo[:, c_cols], w_f[:, c_cols], w_hi[:, c_cols], S["wcl_ready"])
            dve.wait_ge(S["rstd0_ready"], 1)
            for t in (2, 3, 1):
                nc.vector.tensor_scalar(xn[:, t, :], tile_ap(0, t), mv[:, t, 0:1], rstd[:, t:t + 1], ALU.subtract,
                                        ALU.mult).then_inc(S["xn0_dve_ready"], 1)
            dve.wait_ge(S["ah_ready"], 1)
            split_lo(a_lo[:], score[0][:, 0:P], a_hi[:], S["a_ready"])
            early, late = slice(0, 2 * P), slice(2 * P, NT * P)
            dve.wait_ge(S["xh_late_ready"], 1)
            nc.vector.tensor_tensor(xT_lo[:, 0, late], late_x[:, early], xT_hi[:, 0, late].bitcast(F32), ALU.subtract)
            dve.wait_ge(S["xh_ready"], 1)
            split_lo(xT_lo[:, 0, early], bank("X", 0)[:, early], xT_hi[:, 0, early], S["xl_ready"])
            normal_stats(1, 0)
            normal_stats(1, 1)
            normal_stats(1, 2)
            normal_stats(1, 3)
            bias_rhs(0)
            u_lo(0)
            normal_finish(1)
            mask_scores(0, 0)
            negate_max(0, 0)
            gate_max(0)
            gate_below(0)
            weights_lo(0)
            gate_index(0)
            gate_sum(0)
            sv_rows(0, 0)
            gate_chosen(0)
            gate_rec(0)
            gate_picked(0)
            gate_norm(0)
            sv_rows(0, 1)
            gate_out(0)
            sv_rows(0, 2)
            mix_b(0, 0, 0)
            mask_scores(0, 1)
            negate_max(0, 1)
            mix_b(0, 0, 1)
            mix_b(0, 0, 2)
            x_lo(1)
            for n in range(1, B - 1):
                mask_scores(n - 1, 2)
                mix_b(n - 1, 1, 0)
                normal_stats(n + 1, 0)
                mix_b(n - 1, 1, 1)
                negate_max(n - 1, 2)
                mix_b(n - 1, 1, 2)
                normal_stats(n + 1, 1)
                normal_stats(n + 1, 2)
                u_lo(n)
                mask_scores(n - 1, 3)
                mix_b(n - 1, 2, 0)
                negate_max(n - 1, 3)
                mix_b(n - 1, 2, 1)
                normal_stats(n + 1, 3)
                gate_max(n)
                mix_b(n - 1, 3, 0)
                gate_below(n)
                softmax_sum(n - 1)
                mix_b(n - 1, 2, 2)
                softmax_tot(n - 1)
                normal_finish(n + 1)
                gate_index(n)
                mix_b(n - 1, 3, 1)
                gate_sum(n)
                mix_b(n - 1, 3, 2)
                mask_scores(n, 0)
                softmax_rec(n - 1)
                negate_max(n, 0)
                gate_rec(n)
                mask_scores(n, 1)
                negate_max(n, 1)
                gate_chosen(n)
                gate_norm(n)
                gate_picked(n)
                finish_tile(n - 1, 0)
                gate_out(n)
                sv_rows(n, 0)
                sv_rows(n, 1)
                sv_rows(n, 2)
                mix_b(n, 0, 0)
                finish_tile(n - 1, 1)
                mix_b(n, 0, 1)
                finish_tile(n - 1, 2)
                mix_b(n, 0, 2)
                finish_tile(n - 1, 3)
                x_lo(n + 1)
            mix_b(B - 2, 1, 0)
            mix_b(B - 2, 1, 1)
            mask_scores(B - 2, 2)
            mix_b(B - 2, 1, 2)
            negate_max(B - 2, 2)
            u_lo(B - 1)
            mask_scores(B - 2, 3)
            mix_b(B - 2, 2, 0)
            negate_max(B - 2, 3)
            gate_max(B - 1)
            gate_below(B - 1)
            softmax_sum(B - 2)
            mix_b(B - 2, 2, 1)
            mix_b(B - 2, 2, 2)
            softmax_tot(B - 2)
            mask_scores(B - 1, 0)
            gate_index(B - 1)
            negate_max(B - 1, 0)
            mask_scores(B - 1, 1)
            softmax_rec(B - 2)
            mix_b(B - 2, 3, 0)
            mix_b(B - 2, 3, 1)
            gate_sum(B - 1)
            gate_rec(B - 1)
            gate_norm(B - 1)
            mix_b(B - 2, 3, 2)
            gate_chosen(B - 1)
            gate_picked(B - 1)
            negate_max(B - 1, 1)
            finish_tile(B - 2, 0)
            gate_out(B - 1)
            sv_rows(B - 1, 0)
            sv_rows(B - 1, 1)
            sv_rows(B - 1, 2)
            mix_b(B - 1, 0, 0)
            finish_tile(B - 2, 1)
            finish_tile(B - 2, 2)
            mix_b(B - 1, 0, 1)
            finish_tile(B - 2, 3)
            mix_b(B - 1, 1, 0)
            mix_b(B - 1, 0, 2)
            mask_scores(B - 1, 2)
            mix_b(B - 1, 2, 0)
            negate_max(B - 1, 2)
            mix_b(B - 1, 1, 1)
            mix_b(B - 1, 1, 2)
            mask_scores(B - 1, 3)
            negate_max(B - 1, 3)
            mix_b(B - 1, 3, 0)
            mix_b(B - 1, 2, 1)
            softmax_sum(B - 1)
            mix_b(B - 1, 2, 2)
            softmax_tot(B - 1)
            softmax_rec(B - 1)
            mix_b(B - 1, 3, 1)
            mix_b(B - 1, 3, 2)
            finish_tile(B - 1, 0)
            finish_tile(B - 1, 1)
            finish_tile(B - 1, 2)
            finish_tile(B - 1, 3)

        @block.scalar
        def _(act):
            act.dma_start(wqk_s[:], w_attention).then_inc(S["w_att"], 16)
            act.dma_start(be_s[:], be).then_inc(S["w_const"], 16)
            act.dma_start(shapes_s[:], shapes).then_inc(S["w_const"], 16)

            def normalize(b):
                act.wait_ge(S["rstd_ready"], b + 1)
                if b > 0:
                    act.wait_ge(S["xt_done"], b)
                for t in range(NT if b > 0 else 1):
                    last = nc.scalar.activation(xn[:, t, :], tile_ap(b, t), ACT.Identity, bias=nmr[:, t:t + 1],
                                                scale=rstd[:, t:t + 1])
                last.then_inc(S["xn_ready"], 1)

            def c_copy(b, t):
                act.wait_ge(S["wide_done"], wide_count("C", b, t))
                if t == 0 and b > 1:
                    act.wait_ge(S["pv_done"], (b - 1) * NT)
                    act.wait_ge(S["sv_done"], b - 1)
                    act.wait_ge(S["y7_ready"], b - 1)
                nc.scalar.copy(c_s[:, b % 2, t, :], bank(f"C{t}", b)[:, 0:COLS["C"]]).then_inc(S["c_used"], 1)

            def gate_exp(b):
                act.wait_ge(S["below_ready"], b + 1)
                if b > 0:
                    act.wait_ge(S["gate_ready"], b)
                nc.scalar.activation(gexp[:], below[:], ACT.Exp).then_inc(S["gexp_ready"], 1)

            def scale_experts(b, t):
                if t == 0:
                    act.wait_ge(S["gate_ready"], b + 1)
                if b > 0:
                    act.wait_ge(S["ffn_ready"], (b - 1) * NT + t + 1)
                act.wait_ge(S["wide_done"], wide_count("A", b, t))
                for e in range(4):
                    last = nc.scalar.mul(ysc[:, t, e, :], bank(f"A{t}", b)[:, e * P:(e + 1) * P], gate[:, b % 2, t, e:e + 1])
                last.then_inc(S["a_used"], 1)

            def softmax_exp(b, t):
                act.wait_ge(S["nmx_ready"], b * NT + t + 1)
                if b > 0:
                    act.wait_ge(S["pt_done"], (b - 1) * NT + t + 1)
                if t == 0 and b > 1:
                    act.wait_ge(S["tot_ready"], b - 1)
                n = (t + 1) * P
                nc.scalar.activation(prob[:, t, 0:n], score_bank(b, t)[:, 0:n], ACT.Exp, bias=nmx[:, b % 2, t:t + 1],
                                     scale=1.0, accum_out=rs[:, b % 2, t:t + 1]).then_inc(S["exp_done"], 1)

            def masked_exp(b):
                act.wait_ge(S["nmx_ready"], b * NT + NT - 1)
                if b > 1:
                    act.wait_ge(S["rows_ready"], b - 1)
                nc.scalar.activation(em[:, b % 2, 0:NT - 1], nmx[:, b % 2, 0:NT - 1], ACT.Exp).then_inc(S["em_done"], 1)

            def probs_copy(b, t):
                act.wait_ge(S["pt_done"], b * NT + t + 1)
                if t == 0 and b > 1:
                    act.wait_ge(S["pv_done"], (b - 1) * NT)
                n = (t + 1) * P
                nc.scalar.copy(probT[:, b % 2, t, 0:n], score_bank(b, t)[:, 0:n]).then_inc(S["pt_ready"], 1)

            def u_hi(b):
                act.wait_ge(S["u_done"], b + 1)
                nc.scalar.copy(uT_hi[:, b % 2, :], bank("U", b)[:]).then_inc(S["uh_ready"], 1)

            def x_hi(b):
                act.wait_ge(S["xt_done"], b + 1)
                if b > 1:
                    act.wait_ge(S["wide_done"], max(wide_count(k, b - 2, NT - 1) for k in "ABC"))
                    act.wait_ge(S["scores_done"], (b - 1) * NT)
                nc.scalar.copy(xT_hi[:, b % 2, :], bank("X", b)[:]).then_inc(S["xh_ready"], 1)

            def biases_hi(b):
                act.wait_ge(S["be_done"], 1)
                nc.scalar.copy(sv_hi[:], attb[:, 0:P]).then_inc(S["beh_ready"], 1)

            def sv_high(b):
                act.wait_ge(S["sv_done"], b + 1)
                if b == 0:
                    act.wait_ge(S["be_ready"], 1)
                if b > 0:
                    act.wait_ge(S["sv_rows_ready"], b)
                nc.scalar.copy(sv_hi[:], bank("SV", b)[:, 0:P]).then_inc(S["svh_ready"], 1)

            def rows_copy(b):
                act.wait_ge(S["dt_done"], b + 1)
                if b > 0:
                    act.wait_ge(S["bias_done"], b)
                nc.scalar.copy(lhsT_rows[:], bank("DT", b)[:, 0:P]).then_inc(S["dt_ready"], 1)

            act.wait_ge(S["ones_ready"], 1)
            nc.scalar.activation(warm[:], ones[:, 0, 0, 0:1], ACT.Exp)
            act.wait_ge(S["w_moe"], 16)
            nc.scalar.copy(w_hi[:, c_cols], w_f[:, c_cols]).then_inc(S["wc_ready"], 1)
            act.wait_ge(S["a_done"], 1)
            nc.scalar.copy(a_hi[:], score[0][:, 0:P]).then_inc(S["ah_ready"], 1)
            nc.scalar.copy(w_hi[:, b_cols], w_f[:, b_cols]).then_inc(S["wb_ready"], 1)
            normalize(0)
            early, late = slice(0, 2 * P), slice(2 * P, NT * P)
            act.wait_ge(S["xt_late_done"], 1)
            nc.scalar.copy(xT_hi[:, 0, late], late_x[:, early]).then_inc(S["xh_late_ready"], 1)
            act.wait_ge(S["xt_done"], 1)
            nc.scalar.copy(xT_hi[:, 0, early], bank("X", 0)[:, early]).then_inc(S["xh_ready"], 1)
            nc.scalar.copy(w_hi[:, a_cols], w_f[:, a_cols]).then_inc(S["wa_ready"], 1)

            biases_hi(0)
            c_copy(0, 0)
            u_hi(0)
            c_copy(0, 1)
            c_copy(0, 2)
            c_copy(0, 3)
            softmax_exp(0, 0)
            sv_high(0)
            probs_copy(0, 0)
            gate_exp(0)
            normalize(1)
            scale_experts(0, 0)
            x_hi(1)
            softmax_exp(0, 1)
            scale_experts(0, 1)
            c_copy(1, 0)
            u_hi(1)
            masked_exp(0)
            c_copy(1, 1)
            c_copy(1, 2)
            probs_copy(0, 1)
            scale_experts(0, 2)
            softmax_exp(0, 2)
            c_copy(1, 3)
            for n in range(1, B - 1):
                softmax_exp(n - 1, 3)
                gate_exp(n)
                probs_copy(n - 1, 2)
                scale_experts(n - 1, 3)
                probs_copy(n - 1, 3)
                sv_high(n)
                rows_copy(n - 1)
                softmax_exp(n, 0)
                normalize(n + 1)
                scale_experts(n, 0)
                x_hi(n + 1)
                probs_copy(n, 0)
                softmax_exp(n, 1)
                scale_experts(n, 1)
                c_copy(n + 1, 0)
                u_hi(n + 1)
                softmax_exp(n, 2)
                probs_copy(n, 1)
                c_copy(n + 1, 1)
                c_copy(n + 1, 2)
                masked_exp(n)
                scale_experts(n, 2)
                c_copy(n + 1, 3)
            softmax_exp(B - 2, 3)
            probs_copy(B - 2, 2)
            scale_experts(B - 2, 3)
            probs_copy(B - 2, 3)
            gate_exp(B - 1)
            softmax_exp(B - 1, 0)
            rows_copy(B - 2)
            sv_high(B - 1)
            scale_experts(B - 1, 0)
            probs_copy(B - 1, 0)
            softmax_exp(B - 1, 1)
            scale_experts(B - 1, 1)
            scale_experts(B - 1, 2)
            probs_copy(B - 1, 1)
            softmax_exp(B - 1, 2)
            masked_exp(B - 1)
            softmax_exp(B - 1, 3)
            probs_copy(B - 1, 2)
            probs_copy(B - 1, 3)
            scale_experts(B - 1, 3)
            rows_copy(B - 1)

        @block.gpsimd
        def _(pool):
            chain = Chain(pool, S["pool_chain"])

            def normal_rstd(b):
                pool.wait_ge(S["veps_ready"], b + 1)
                if b > 0:
                    pool.wait_ge(S["xn_ready"], b)
                if b == 1:
                    pool.wait_ge(S["xn0_dve_ready"], 3)
                power = nc.gpsimd.tensor_tensor(rstd[:], veps[:], half[:], ALU.pow)
                if b == 0:
                    power.then_inc(S["rstd0_ready"], 1)
                    pool.wait_ge(S["rstd0_ready"], 1)
                else:
                    chain.step(power)
                pool.wait_ge(S["nmean_ready"], b + 1)
                nc.gpsimd.tensor_tensor(nmr[:], nmean[:], rstd[:], ALU.mult).then_inc(S["rstd_ready"], 1)

            def scale_last(b):
                pool.wait_ge(S["gate_ready"], b + 1)
                nc.gpsimd.tensor_tensor(y7[:, b % 2, :, :], c_s[:, b % 2, :, Y_AT:Y_AT + P], gate[:, b % 2, :, 7:8].to_broadcast([P, NT, P]),
                                        ALU.mult).then_inc(S["y7_ready"], 1)

            def sum_experts(b, t):
                y = ysc[:, t, :, :]
                pool.wait_ge(S["a_used"], b * NT + t + 1)
                chain.step(nc.gpsimd.tensor_tensor(y[:, 0:2, :], y[:, 0:2, :], y[:, 2:4, :], ALU.add))
                chain.step(nc.gpsimd.tensor_tensor(y[:, 0, :], y[:, 0, :], y[:, 1, :], ALU.add))
                pool.wait_ge(S["y7_ready"], b + 1)
                chain.step(nc.gpsimd.tensor_tensor(y[:, 0, :], y[:, 0, :], y7[:, b % 2, t, :], ALU.add))
                pool.wait_ge(S["mix_ready"], b * NT + t + 1)
                if b > 1:
                    pool.wait_ge(S["fin_done"], (b - 2) * NT + t + 1)
                nc.gpsimd.tensor_tensor(ffn[:, b % 2, t, :], y[:, 0, :], mix[:, t, 2, :], ALU.add
                                        ).then_inc(S["ffn_ready"], 1)

            def bias_rows(b):
                rows3 = lhs_rows[:].rearrange("p (t r) -> p t r", r=ROWS)
                n = NT - 1
                pool.wait_ge(S["em_done"], b + 1)
                pool.wait_ge(S["gate_ready"], b + 1)
                pool.wait_ge(S["tot_ready"], b + 1)
                if b > 0:
                    pool.wait_ge(S["dt_done"], b)
                tot_g = chain.mark(nc.gpsimd.tensor_tensor(gate_tot[:], gate[:, b % 2, :, :], tot[:, b % 2, :].unsqueeze(2).to_broadcast(
                    [P, NT, E]), ALU.mult))
                e_hi = chain.mark(nc.gpsimd.tensor_tensor(rows3[:, 0:n, 0:2], em[:, b % 2, 0:n].unsqueeze(2).to_broadcast(
                    [P, n, 2]), ones[:, 0:n, 0, 0:2], ALU.mult))
                chain.need(tot_g)
                g_hi = chain.mark(nc.gpsimd.tensor_tensor(
                    rows3[:, :, G_ROW:G_ROW + 2 * E].rearrange("p t (c e) -> p t c e", e=E),
                    gate_tot[:].unsqueeze(2).to_broadcast([P, NT, 2, E]), ones[:], ALU.mult))
                chain.need(e_hi)
                nc.gpsimd.tensor_tensor(rows3[:, 0:n, 2], em[:, b % 2, 0:n], rows3[:, 0:n, 0].bitcast(F32), ALU.subtract)
                chain.need(g_hi)
                nc.gpsimd.tensor_tensor(rows3[:, :, G_ROW + 2 * E:G_ROW + 3 * E], gate_tot[:],
                                        rows3[:, :, G_ROW:G_ROW + E].bitcast(F32), ALU.subtract
                                        ).then_inc(S["rows_ready"], 1)

            nc.gpsimd.memset(ones[:], 1.0).then_inc(S["ones_ready"], 1)
            cleared = chain.mark(nc.gpsimd.memset(ident[:], 0.0))
            nc.gpsimd.memset(half[:], -0.5)
            nc.gpsimd.memset(masked_keys[:, 0:1], float(T - P))
            for t in range(1, NT):
                nc.gpsimd.memset(masked_keys[:, t:t + 1], float(T - (t + 1) * P))
            chain.need(cleared)
            nc.gpsimd.affine_select(out=ident[:], in_=ident[:], compare_op=ALU.not_equal, fill=1.0, base=0,
                                    pattern=[[-1, P]], channel_multiplier=1).then_inc(S["ident_ready"], 1)
            nc.gpsimd.iota(iota8[:], pattern=[[1, E]], base=0, channel_multiplier=0,
                           allow_small_or_imprecise_dtypes=True)
            nc.gpsimd.memset(em[:], 0.0)
            full = chain.mark(nc.gpsimd.memset(causal[:], 1.0))
            cleared = chain.mark(nc.gpsimd.memset(suffix[:], 0.0))
            chain.need(full)
            nc.gpsimd.affine_select(out=causal[:, (NT - 1) * P:], in_=causal[:, (NT - 1) * P:], compare_op=ALU.is_ge, fill=0.0, base=0,
                                    pattern=[[-1, P]], channel_multiplier=1)
            chain.need(cleared)
            for m in range(1, NT):
                v = suffix[:, m, :].rearrange("p (t r) -> p t r", r=ROWS)
                last = nc.gpsimd.memset(v[:, 0:m, 0:G_ROW], 1.0)
            chain.step(last)
            normal_rstd(0)
            pool.wait_ge(S["wb_ready"], 1)
            nc.gpsimd.tensor_tensor(w_lo[:, b_cols], w_f[:, b_cols], w_hi[:, b_cols].bitcast(F32), ALU.subtract
                                    ).then_inc(S["wlb_ready"], 1)
            nc.gpsimd.memset(lhs_rows[:].bitcast(F32), 0.0)
            chain.step(nc.gpsimd.memset(rhs_rows[:].bitcast(F32), 0.0))
            pool.sem_inc(S["consts_ready"], 1)

            normal_rstd(1)
            scale_last(0)
            sum_experts(0, 0)
            sum_experts(0, 1)
            sum_experts(0, 2)
            bias_rows(0)
            for n in range(1, B - 1):
                normal_rstd(n + 1)
                sum_experts(n - 1, 3)
                scale_last(n)
                sum_experts(n, 0)
                sum_experts(n, 1)
                sum_experts(n, 2)
                bias_rows(n)
            sum_experts(B - 2, 3)
            scale_last(B - 1)
            sum_experts(B - 1, 0)
            sum_experts(B - 1, 1)
            sum_experts(B - 1, 2)
            bias_rows(B - 1)
            sum_experts(B - 1, 3)


_INS = ['L0_attn_x', 'L0_attn_Wq', 'L0_attn_Wk', 'L0_attn_Wv', 'L0_ffn_Wg', 'L0_ffn_We', 'L0_ffn_be']
_OUT = ((8, 512, 128), 'float32')


def kernel(**inputs):
    import numpy as _np
    import concourse.bacc as _bacc
    from concourse import mybir as _mybir
    from concourse.bass_utils import run_bass_kernel_spmd as _run

    nc = _bacc.Bacc("TRN2", target_bir_lowering=False, num_devices=1)
    arrays, args = {}, []
    x, wq, wk, wv, wg, we, be = (inputs[name] for name in _INS)
    arrays["in_x_dram"] = _np.ascontiguousarray(x)
    arrays["in_w_attention_dram"] = _np.concatenate([wq, wk], axis=1)
    arrays["in_w_stacked_dram"] = _np.concatenate([_np.transpose(wv), we[7], wg] + [we[e] for e in range(7)], axis=1)
    arrays["in_be_dram"] = _np.ascontiguousarray(be)
    r = _np.arange(P) % ROWS
    shapes = _np.zeros((P, P + 1), _np.float32)
    shapes[0:8, 0:P] = ((r - G_ROW)[None, :] % 8 == _np.arange(8)[:, None]) & (r >= G_ROW) & (r < G_ROW + 24)
    shapes[:, P] = _np.where(((r >= G_ROW + 8) & (r < G_ROW + 16)) | (r == 1), -1.0, 0.0)
    arrays["in_shapes_dram"] = shapes
    for k, a in arrays.items():
        args.append(nc.dram_tensor(k, a.shape, _mybir.dt.from_np(a.dtype), kind="ExternalInput").ap())
    shape, dtype = _OUT
    o = nc.dram_tensor("out_0_dram", shape, _mybir.dt.from_np(_np.dtype(dtype)), kind="ExternalOutput").ap()
    build(nc, *args, o)
    return _run(nc, [arrays], core_ids=[0]).results[0]["out_0_dram"]
```
